# Optimizing a Trainium2 kernel written in Bass

```python
import numpy as np
import jax
import jax.numpy as jnp

def _softmax(x, axis=-1):
    return jax.nn.softmax(x, axis=axis)

def _gelu(x):
    return jax.nn.gelu(x, approximate=True)

def _silu(x):
    return jax.nn.silu(x)

def _sigmoid(x):
    return jax.nn.sigmoid(x)

def _layernorm(x, axis=-1, eps=1e-05):
    m = jnp.mean(x, axis=axis, keepdims=True)
    v = jnp.var(x, axis=axis, keepdims=True)
    return (x - m) / jnp.sqrt(v + eps)

def _scatter_add(tgt, idx, src, axis=0):
    return tgt.at[idx].add(src)

def _segment_sum(src, seg, n):
    return jax.ops.segment_sum(src, seg, n)
kernel_name = 'mk_adj_ffn_d1_adj_r2_538034'

def setup_inputs(seed: int=0):
    np.random.seed(seed)
    _w = jnp.asarray

    def _rec_inputs():
        import jax
        import jax.numpy as jnp
        _gk = jax.random.key(seed)
        x = -0.0002928 + 1 * jax.random.normal(jax.random.fold_in(_gk, 1), (2048, 256), jnp.float32)
        _a = jax.random.bernoulli(jax.random.fold_in(_gk, 2), 0.000976562, (2048, 2048))
        _a = jnp.logical_or(_a, jnp.swapaxes(_a, -1, -2))
        _a = jnp.logical_or(_a, jnp.eye(2048, dtype=bool))
        _af = _a.astype(jnp.float32)
        _af = _af * jax.random.uniform(jax.random.fold_in(_gk, 3), (2048, 2048), jnp.float32, 0.05, 1)
        adj = _af
        return (x, adj)
    x, adj = _rec_inputs()

    def _L0_gnn_setup():
        import jax, jax.numpy as jnp
        import numpy as np
        N = 4096
        D_IN = 256
        D_OUT = 256
        key = jax.random.key(seed)
        k1, k2, k3, k4 = jax.random.split(key, 4)
        x = jax.random.normal(k1, (N, D_IN), dtype=jnp.float32)
        adj = jax.random.uniform(k2, (N, N), dtype=jnp.float32)
        bound = 1.0 / np.sqrt(D_IN)
        W = jax.random.uniform(k3, (D_OUT, D_IN), minval=-bound, maxval=bound, dtype=jnp.float32)
        b = jax.random.uniform(k4, (D_OUT,), minval=-bound, maxval=bound, dtype=jnp.float32)
        return {'x': x, 'adj': adj, 'W': W, 'b': b}
    _L0_gnn_all = _L0_gnn_setup()
    _L0_gnn_in = {k: v for k, v in _L0_gnn_all.items() if k in ('W', 'b')}
    del _L0_gnn_all

    def _L0_ffn_setup():
        import jax, jax.numpy as jnp
        import numpy as np
        D_MODEL, D_IN, N, DT_RANK, K, E = (256, 512, 16, 32, 4, 8)
        B, L = (4, 512)
        EPS = 1e-05

        def rmsnorm(x, w):
            return x * jax.lax.rsqrt(jnp.mean(jnp.square(x), axis=-1, keepdims=True) + EPS) * w

        def selective_scan(u, delta, A, Bm, Cm, Dp):
            dA = jnp.einsum('bld,dn->bldn', delta, A)
            dBu = jnp.einsum('bld,bld,bln->bldn', delta, u, Bm)
            dA_shift = jnp.concatenate([dA[:, 1:], jnp.zeros_like(dA[:, :1])], axis=1)
            dA_cs = jnp.exp(jnp.flip(jnp.cumsum(jnp.flip(dA_shift, axis=1), axis=1), axis=1))
            x = jnp.cumsum(dBu * dA_cs, axis=1) / (dA_cs + 1e-12)
            y = jnp.einsum('bldn,bln->bld', x, Cm)
            return y + u * Dp

        def mamba_block(x, W_in, conv_w, conv_b, W_x, W_dt, b_dt, A_log, Dp, W_out):
            xr = x @ W_in
            xs, res = (xr[..., :D_IN], xr[..., D_IN:])
            xc = jnp.transpose(xs, (0, 2, 1))
            xc = jax.lax.conv_general_dilated(xc, conv_w, window_strides=(1,), padding=[(K - 1, 0)], dimension_numbers=('NCH', 'OIH', 'NCH'), feature_group_count=D_IN)
            xc = xc + conv_b[None, :, None]
            xs = jax.nn.silu(jnp.transpose(xc, (0, 2, 1)))
            x_dbl = xs @ W_x
            dt = x_dbl[..., :DT_RANK]
            Bm = x_dbl[..., DT_RANK:DT_RANK + N]
            Cm = x_dbl[..., DT_RANK + N:]
            delta = jax.nn.softplus(dt @ W_dt + b_dt)
            A = -jnp.exp(A_log)
            y = selective_scan(xs, delta, A, Bm, Cm, Dp)
            y = y * jax.nn.silu(res)
            return y @ W_out

        def moe(x, W_gate, W1, b1, W2, b2):
            g = jax.nn.softmax(x @ W_gate, axis=-1)
            h = jax.nn.silu(jnp.einsum('bld,edh->bleh', x, W1) + b1)
            o = jnp.einsum('bleh,ehd->bled', h, W2) + b2
            return jnp.einsum('ble,bled->bld', g, o)
        key = jax.random.key(seed)
        ks = jax.random.split(key, 10)
        s = 0.02
        return {'inputs': jax.random.normal(ks[0], (B, L, D_MODEL), jnp.float32), 'w_rms1': jnp.ones((D_MODEL,), jnp.float32), 'w_rms2': jnp.ones((D_MODEL,), jnp.float32), 'W_in': jax.random.normal(ks[1], (D_MODEL, 2 * D_IN), jnp.float32) * s, 'conv_w': jax.random.normal(ks[2], (D_IN, 1, K), jnp.float32) * s, 'conv_b': jnp.zeros((D_IN,), jnp.float32), 'W_x': jax.random.normal(ks[3], (D_IN, DT_RANK + 2 * N), jnp.float32) * s, 'W_dt': jax.random.normal(ks[4], (DT_RANK, D_IN), jnp.float32) * s, 'b_dt': jnp.zeros((D_IN,), jnp.float32), 'A_log': jnp.log(jnp.broadcast_to(jnp.arange(1, N + 1, dtype=jnp.float32), (D_IN, N)) + 0.0), 'Dp': jnp.ones((D_IN,), jnp.float32), 'W_out': jax.random.normal(ks[5], (D_IN, D_MODEL), jnp.float32) * s, 'W_gate': jax.random.normal(ks[6], (D_MODEL, E), jnp.float32) * s, 'W1': jax.random.normal(ks[7], (E, D_MODEL, D_IN), jnp.float32) * s, 'b1': jnp.zeros((E, D_IN), jnp.float32), 'W2': jax.random.normal(ks[8], (E, D_IN, D_MODEL), jnp.float32) * s, 'b2': jnp.zeros((E, D_MODEL), jnp.float32)}
    _L0_ffn_all = _L0_ffn_setup()
    _L0_ffn_in = {k: v for k, v in _L0_ffn_all.items() if k in ('w_rms1', 'w_rms2', 'W_in', 'conv_w', 'conv_b', 'W_x', 'W_dt', 'b_dt', 'A_log', 'Dp', 'W_out', 'W_gate', 'W1', 'b1', 'W2', 'b2')}
    del _L0_ffn_all
    return {'x': x, 'adj': adj, 'L0_gnn_W': _L0_gnn_in['W'], 'L0_gnn_b': _L0_gnn_in['b'], 'L0_ffn_w_rms1': _L0_ffn_in['w_rms1'], 'L0_ffn_w_rms2': _L0_ffn_in['w_rms2'], 'L0_ffn_W_in': _L0_ffn_in['W_in'], 'L0_ffn_conv_w': _L0_ffn_in['conv_w'], 'L0_ffn_conv_b': _L0_ffn_in['conv_b'], 'L0_ffn_W_x': _L0_ffn_in['W_x'], 'L0_ffn_W_dt': _L0_ffn_in['W_dt'], 'L0_ffn_b_dt': _L0_ffn_in['b_dt'], 'L0_ffn_A_log': _L0_ffn_in['A_log'], 'L0_ffn_Dp': _L0_ffn_in['Dp'], 'L0_ffn_W_out': _L0_ffn_in['W_out'], 'L0_ffn_W_gate': _L0_ffn_in['W_gate'], 'L0_ffn_W1': _L0_ffn_in['W1'], 'L0_ffn_b1': _L0_ffn_in['b1'], 'L0_ffn_W2': _L0_ffn_in['W2'], 'L0_ffn_b2': _L0_ffn_in['b2']}

def reference(x, adj, L0_gnn_W, L0_gnn_b, L0_ffn_w_rms1, L0_ffn_w_rms2, L0_ffn_W_in, L0_ffn_conv_w, L0_ffn_conv_b, L0_ffn_W_x, L0_ffn_W_dt, L0_ffn_b_dt, L0_ffn_A_log, L0_ffn_Dp, L0_ffn_W_out, L0_ffn_W_gate, L0_ffn_W1, L0_ffn_b1, L0_ffn_W2, L0_ffn_b2):
    import jax
    import jax.numpy as jnp

    def _L0_gnn_ref(x, adj, W, b):
        import jax, jax.numpy as jnp
        import numpy as np
        N = 4096
        D_IN = 256
        D_OUT = 256
        a = adj + jnp.eye(adj.shape[0], dtype=adj.dtype)
        d = jnp.sum(a, axis=1) ** (-0.5)
        a_norm = d[:, None] * a * d[None, :]
        support = a_norm @ x
        out = support @ W.T + b
        out = jax.nn.relu(out)
        return out

    def _L0_ffn_ref(inputs, w_rms1, w_rms2, W_in, conv_w, conv_b, W_x, W_dt, b_dt, A_log, Dp, W_out, W_gate, W1, b1, W2, b2):
        import jax, jax.numpy as jnp
        import numpy as np
        D_MODEL, D_IN, N, DT_RANK, K, E = (256, 512, 16, 32, 4, 8)
        B, L = (4, 512)
        EPS = 1e-05

        def rmsnorm(x, w):
            return x * jax.lax.rsqrt(jnp.mean(jnp.square(x), axis=-1, keepdims=True) + EPS) * w

        def selective_scan(u, delta, A, Bm, Cm, Dp):
            dA = jnp.einsum('bld,dn->bldn', delta, A)
            dBu = jnp.einsum('bld,bld,bln->bldn', delta, u, Bm)
            dA_shift = jnp.concatenate([dA[:, 1:], jnp.zeros_like(dA[:, :1])], axis=1)
            dA_cs = jnp.exp(jnp.flip(jnp.cumsum(jnp.flip(dA_shift, axis=1), axis=1), axis=1))
            x = jnp.cumsum(dBu * dA_cs, axis=1) / (dA_cs + 1e-12)
            y = jnp.einsum('bldn,bln->bld', x, Cm)
            return y + u * Dp

        def mamba_block(x, W_in, conv_w, conv_b, W_x, W_dt, b_dt, A_log, Dp, W_out):
            xr = x @ W_in
            xs, res = (xr[..., :D_IN], xr[..., D_IN:])
            xc = jnp.transpose(xs, (0, 2, 1))
            xc = jax.lax.conv_general_dilated(xc, conv_w, window_strides=(1,), padding=[(K - 1, 0)], dimension_numbers=('NCH', 'OIH', 'NCH'), feature_group_count=D_IN)
            xc = xc + conv_b[None, :, None]
            xs = jax.nn.silu(jnp.transpose(xc, (0, 2, 1)))
            x_dbl = xs @ W_x
            dt = x_dbl[..., :DT_RANK]
            Bm = x_dbl[..., DT_RANK:DT_RANK + N]
            Cm = x_dbl[..., DT_RANK + N:]
            delta = jax.nn.softplus(dt @ W_dt + b_dt)
            A = -jnp.exp(A_log)
            y = selective_scan(xs, delta, A, Bm, Cm, Dp)
            y = y * jax.nn.silu(res)
            return y @ W_out

        def moe(x, W_gate, W1, b1, W2, b2):
            g = jax.nn.softmax(x @ W_gate, axis=-1)
            h = jax.nn.silu(jnp.einsum('bld,edh->bleh', x, W1) + b1)
            o = jnp.einsum('bleh,ehd->bled', h, W2) + b2
            return jnp.einsum('ble,bled->bld', g, o)
        x = rmsnorm(inputs, w_rms1)
        x = mamba_block(x, W_in, conv_w, conv_b, W_x, W_dt, b_dt, A_log, Dp, W_out)
        x1 = x + inputs
        x = rmsnorm(x1, w_rms2)
        x = moe(x, W_gate, W1, b1, W2, b2)
        return x + x1
    x = x + _L0_gnn_ref(_layernorm(x, axis=-1), adj, L0_gnn_W, L0_gnn_b)
    x = x + _L0_ffn_ref(_layernorm(x, axis=-1)[None], L0_ffn_w_rms1, L0_ffn_w_rms2, L0_ffn_W_in, L0_ffn_conv_w, L0_ffn_conv_b, L0_ffn_W_x, L0_ffn_W_dt, L0_ffn_b_dt, L0_ffn_A_log, L0_ffn_Dp, L0_ffn_W_out, L0_ffn_W_gate, L0_ffn_W1, L0_ffn_b1, L0_ffn_W2, L0_ffn_b2)[0]
    return x

_drawn_inputs = setup_inputs


def setup_inputs(seed=0):
    import zlib

    import numpy as np

    out = dict(_drawn_inputs(seed))
    spreads = {'L0_ffn_w_rms1': (1.0, 0.6),
     'L0_ffn_w_rms2': (1.0, 0.6),
     'L0_ffn_conv_b': (0.0, 0.8),
     'L0_ffn_b_dt': (0.0, 0.8),
     'L0_ffn_Dp': (1.0, 0.6),
     'L0_ffn_b1': (0.0, 0.8),
     'L0_ffn_b2': (0.0, 1.98)}
    factors = {'L0_ffn_W_in': 8.0,
     'L0_ffn_conv_w': 8.0,
     'L0_ffn_W_x': 8.0,
     'L0_ffn_W_dt': 8.0,
     'L0_ffn_A_log': 8.0,
     'L0_ffn_W_out': 8.0,
     'L0_ffn_W_gate': 7.726,
     'L0_ffn_W1': 3.905,
     'L0_ffn_W2': 3.673}
    for name, (base, spread) in spreads.items():
        noise = np.random.default_rng([zlib.crc32(name.encode()), seed]).standard_normal(out[name].shape)
        drawn = base * np.exp(spread * noise) if base else spread * noise
        out[name] = jnp.asarray(drawn.astype(out[name].dtype))
    for name, factor in factors.items():
        out[name] = (out[name] * factor).astype(out[name].dtype)
    return out
```

```python
import math
from contextlib import ExitStack

import concourse.bass as bass
from concourse import mybir

F32 = mybir.dt.float32
ALU = mybir.AluOpType
ACT = mybir.ActivationFunctionType
AX = mybir.AxisListType.X

P = 128
BLK = 512
EPS = 1e-5
SCAN_EPS = 1e-12


def await_ge(eng, sem, value):
    eng.wait_ge(sem, value)
    if not isinstance(value, int):
        eng.nop(nofuse=True)


class Steps:

    def __init__(self, eng, sem, start):
        self.eng, self.sem, self.n, self.start = eng, sem, 0, start

    def did(self, ins):
        ins.then_inc(self.sem, 1)
        self.n += 1

    def wait(self, back=0):
        await_ge(self.eng, self.sem, self.start + (self.n - back))


def build(nc, x, adj, gnn_w, gnn_b, w_rms1, w_rms2, w_in, conv_w, conv_b, w_x, w_dt, b_dt, a_log,
          d_skip, w_out, w_gate, w1, b1, w2, b2, out):
    L, D = x.shape
    DI = w_out.shape[0]
    NS = a_log.shape[1]
    DTR = w_dt.shape[0]
    NE = w_gate.shape[1]
    NT = L // P
    NB = L // BLK
    TB = BLK // P
    CD = D // P
    CI = DI // P
    XD = DTR + 2 * NS
    assert (CD, CI, TB, NB, NS, NE, XD) == (2, 4, 4, 4, 16, 8, 64)

    gnn_rows = nc.dram_tensor("gnn_rows", [L, D], F32, kind="Internal").ap()
    norm_rows = nc.dram_tensor("norm_rows", [L, D], F32, kind="Internal").ap()
    bc_rows = nc.dram_tensor("bc_rows", [2 * NS, L], F32, kind="Internal").ap()
    bc_pairs = bc_rows.rearrange("(a n) l -> n a l", a=2)
    adj_t = adj.rearrange("(t p) j -> t p j", p=P)

    ctx = ExitStack()
    with ctx:
        def sb(name, shape):
            return ctx.enter_context(nc.sbuf_tensor(name, shape, F32))

        def sem(name):
            return ctx.enter_context(nc.semaphore(name))

        arena = sb("arena", [P, NB, NT, BLK])
        U0, G0, D0, S0 = 0, CI, 2 * CI, 3 * CI
        low = sb("low", [P, 22016])

        def view(at, *dims):
            n = math.prod(dims)
            v = low[:, at:at + n]
            if len(dims) == 2:
                v = v.rearrange("p (a b) -> p a b", a=dims[0])
            elif len(dims) == 3:
                v = v.rearrange("p (a b c) -> p a b c", a=dims[0], b=dims[1])
            return v

        xrow = view(0, NT, D)
        z = view(4096, NT, D)
        wnat = view(4096, CD, D)
        ring = view(8192, 4, L)
        normed = view(8192, TB, D)
        pre = view(9216, TB, D)
        gT = view(10240, CD, BLK)
        preT = view(11264, CD, BLK)
        stage = view(12288, CI, BLK + 4)
        xdbl = view(14400, BLK)
        win_sb = view(16384, CD, 2 * DI)
        wT = view(18432, CD, D)
        gb_bc = view(18944, D)
        wx_sb = view(19200, CI, XD)
        wdt_sb = view(19456, DI)
        wout_sb = view(19968, CI, D)
        ones = view(20992, BLK)
        rsum = view(0, CI, BLK)
        bu = view(2048, 2, 2, BLK)
        bc = view(4096, 2, 2, BLK)
        gate = view(6144, 2, 2, BLK)
        gate_all = view(6144, CI, BLK)
        yc = view(8192, 2, 2, BLK)
        hT = view(10240, CI, BLK)
        xmT = view(12288, CD, BLK)
        w1_sb = view(13312, 2, CD * DI)
        w2_sb = view(15360, 2, CI * D)
        acc = view(17408, TB, D)
        xm = view(18432, TB, D)
        gateT = view(19456, BLK)

        ident = sb("ident", [P, P])
        rowsum = sb("rowsum", [P, NT])
        deg = sb("deg", [P, NT])
        stats = sb("stats", [P, NT, 6])
        mv = sb("mv", [P, NT, 2])
        sa, sb_, sc_, sd_ = (sb(f"small{i}", [P, NT]) for i in range(4))
        zscale = sb("zscale", [P, NT])
        zbias = sb("zbias", [P, NT])
        stats2 = sb("stats2", [P, TB, 6])
        mv2 = sb("mv2", [P, TB, 2])
        q = sb("q", [P, 2 * TB])
        qr = sb("qr", [P, 2 * TB])
        qt = sb("qt", [P, 2 * TB])
        VECS = 2 * CD + 3 * CI + NE * CI
        vec_rows = sb("vec_rows", [VECS, P])
        vecs = sb("vecs", [P, VECS])
        w1c, w2c = vecs[:, 0:CD], vecs[:, CD:2 * CD]
        cb, bdt, dp = (vecs[:, 2 * CD + i * CI:2 * CD + (i + 1) * CI] for i in range(3))
        B1 = 2 * CD + 3 * CI
        cw = sb("cw", [P, CI, 4])
        amat = sb("amat", [P, CI, NS])
        ahalf = sb("ahalf", [P, CI, NS])
        carry = sb("carry", [P, CI, NS])
        tot = sb("tot", [P, CI, NB])
        suffix = sb("suffix", [P, CI, NB])
        eps_c = sb("eps_c", [P, 1])
        guard_c = sb("guard_c", [P, 1])
        wg_sb = sb("wg_sb", [P, CD, NE])
        b2_sb = sb("b2_sb", [NE, D])
        ss = sb("ss", [P, TB])
        ssv = sb("ssv", [P, TB])
        r2 = sb("r2", [P, TB])
        r2t = sb("r2t", [P, TB])
        gw = sb("gw", [P, TB, NE])
        gmax = sb("gmax", [P, TB])
        gsum = sb("gsum", [P, TB])

        ps = ctx.enter_context(nc.psum_tensor("ps", [P, 8, BLK], F32))

        consts_loaded = sem("consts_loaded")
        x_loaded = sem("x_loaded")
        adj_loaded = [sem(f"adj_loaded{i}") for i in range(4)]
        pool_made = sem("pool_made")
        w_turned = sem("w_turned")
        w_kept = sem("w_kept")
        diag_added = sem("diag_added")
        row_summed = sem("row_summed")
        adj_turned = sem("adj_turned")
        adj_kept = sem("adj_kept")
        dve_a = sem("dve_a")
        act_a = sem("act_a")
        roots_a = sem("roots_a")
        z_made = sem("z_made")
        gcn_done = sem("gcn_done")
        gT_kept = sem("gT_kept")
        wmm_done = sem("wmm_done")
        q_made = sem("q_made")
        q_rooted = sem("q_rooted")
        dve_b = sem("dve_b")
        x1_made = sem("x1_made")
        pre_made = sem("pre_made")
        pre_turned = sem("pre_turned")
        preT_kept = sem("preT_kept")
        inproj_done = sem("inproj_done")
        inproj_used = sem("inproj_used")
        conv_done = sem("conv_done")
        u_made = sem("u_made")
        xdbl_done = sem("xdbl_done")
        xdbl_kept = sem("xdbl_kept")
        dt_done = sem("dt_done")
        act_soft = sem("act_soft")
        soft_made = sem("soft_made")
        delta_made = sem("delta_made")
        dt_abs = sem("dt_abs")
        dt_relu = sem("dt_relu")
        rows_saved = sem("rows_saved")
        bc_saved = sem("bc_saved")
        phase_a = sem("phase_a")
        skip_made = sem("skip_made")
        r_made = sem("r_made")
        dve_r = sem("dve_r")
        dve_c = sem("dve_c")
        bc_loaded = [sem(f"bc_loaded{i}") for i in range(2)]
        bu_made = sem("bu_made")
        a_made = sem("a_made")
        gate_made = sem("gate_made")
        scanned = sem("scanned")
        carried = sem("carried")
        guarded = sem("guarded")
        weighted = sem("weighted")
        summed = sem("summed")
        wt_loaded = [sem(f"wt_loaded{i}") for i in range(2)]
        normed_loaded = sem("normed_loaded")
        gnn_loaded = sem("gnn_loaded")
        yg_made = sem("yg_made")
        mamba_done = sem("mamba_done")
        dve_p = sem("dve_p")
        v_made = sem("v_made")
        ss_made = sem("ss_made")
        ss_rooted = sem("ss_rooted")
        xm_made = sem("xm_made")
        xm_turned = sem("xm_turned")
        xmT_kept = sem("xmT_kept")
        gate_done = sem("gate_done")
        logit_made = sem("logit_made")
        gexp_made = sem("gexp_made")
        gw_made = sem("gw_made")
        gw_turned = sem("gw_turned")
        gateT_kept = sem("gateT_kept")
        b2_done = sem("b2_done")
        b2_used = sem("b2_used")
        hid_done = sem("hid_done")
        hid_kept = sem("hid_kept")
        exp_done = sem("exp_done")
        exp_used = sem("exp_used")
        acc_done = sem("acc_done")
        out_saved = sem("out_saved")

        block = ctx.enter_context(nc.Block())

        NP_CHUNK = NS * 2
        CONSTS = 16

        def xrow_block(k):
            return low[:, bass.ds(k * (TB * D), TB * D)].rearrange("p (t d) -> p t d", t=TB)

        @block.sync
        def _(sync):
            def const(to, of):
                sync.dma_start(to, of).then_inc(consts_loaded, 16)

            sync.dma_start(xrow, x.rearrange("(t p) d -> p t d", p=P)).then_inc(x_loaded, 16)

            def load_adj(t, s, first):
                if not first:
                    await_ge(sync, row_summed, t - 3)
                    await_ge(sync, adj_turned, 4 * (t - 3))
                sync.dma_start(ring[:, s, :], adj_t[t, :, :]).then_inc(adj_loaded[s], 16)

            for s in range(4):
                load_adj(s, s, True)
            const(wnat, gnn_w.rearrange("(a p) c -> p a c", p=P))
            const(win_sb, w_in.rearrange("(a p) n -> p a n", p=P))
            const(wx_sb, w_x.rearrange("(a p) n -> p a n", p=P))
            const(wdt_sb[0:DTR, :], w_dt)
            const(wout_sb, w_out.rearrange("(a p) n -> p a n", p=P))
            const(gb_bc, gnn_b.partition_broadcast(P))
            at = 0
            for v in (w_rms1, w_rms2, conv_b, b_dt, d_skip, b1.rearrange("e n -> (e n)")):
                rows = v.shape[0] // P
                const(vec_rows[at:at + rows, :], v.rearrange("(a p) -> a p", p=P))
                at += rows
            const(cw[:, :, :], conv_w.rearrange("(a p) o k -> p a (o k)", p=P))
            const(amat[:, :, :], a_log.rearrange("(a p) n -> p a n", p=P))
            const(wg_sb[:, :, :], w_gate.rearrange("(a p) n -> p a n", p=P))
            const(b2_sb[:, :], b2)
            with sync.Fori(1, NT // 4) as it:
                for s in range(4):
                    load_adj(4 * it + s, s, False)

            def save(k):
                await_ge(sync, x1_made, k + 1)
                sync.dma_start(gnn_rows.rearrange("(k t p) d -> k p t d", p=P, t=TB)[k],
                               xrow_block(k)).then_inc(rows_saved, 16)
                await_ge(sync, pre_made, TB * (k + 1))
                sync.dma_start(norm_rows.rearrange("(k t p) d -> k p t d", p=P, t=TB)[k],
                               normed).then_inc(rows_saved, 16)
                await_ge(sync, xdbl_kept, k + 1)
                sync.dma_start(bc_rows.rearrange("n (k l) -> k n l", k=NB)[k],
                               xdbl[DTR:XD, :]).then_inc(bc_saved, 16)

            with sync.Fori(0, NB) as k:
                save(k)

            await_ge(sync, bc_saved, 16 * NB)
            await_ge(sync, rows_saved, 32 * NB)
            sync.wait_ge(phase_a, 4)

            def load_bc(c, n, s, first):
                if not first:
                    await_ge(sync, bu_made, NP_CHUNK * c + 2 * (n - 1))
                    await_ge(sync, weighted, NP_CHUNK * c + 2 * (n - 1))
                sync.dma_start(bc[:, s, :, :],
                               bc_rows.rearrange("(a n) (k l) -> k n a l", a=2, k=NB)[c, n]
                               .partition_broadcast(P)).then_inc(bc_loaded[s], 16)

            def load_expert(c, e, s, first):
                if not first:
                    await_ge(sync, exp_done, 4 * (NE * c + e - 1))
                sync.dma_start(w1_sb[:, s, :].rearrange("p (a n) -> p a n", a=CD),
                               w1.rearrange("e (a p) n -> e p a n", p=P)[e]).then_inc(wt_loaded[s], 16)
                sync.dma_start(w2_sb[:, s, :].rearrange("p (a n) -> p a n", a=CI),
                               w2.rearrange("e (a p) n -> e p a n", p=P)[e]).then_inc(wt_loaded[s], 16)

            def load_rows(c, first):
                if not first:
                    await_ge(sync, out_saved, 16 * c)
                sync.dma_start(acc, norm_rows.rearrange("(k t p) d -> k p t d", p=P, t=TB)[c])\
                    .then_inc(normed_loaded, 16)

            def load_gnn(c):
                await_ge(sync, xm_turned, c + 1)
                sync.dma_start(xm, gnn_rows.rearrange("(k t p) d -> k p t d", p=P, t=TB)[c])\
                    .then_inc(gnn_loaded, 16)

            def store(c):
                await_ge(sync, acc_done, c + 1)
                sync.dma_start(out.rearrange("(k t p) d -> k p t d", p=P, t=TB)[c], acc)\
                    .then_inc(out_saved, 16)

            for n in range(2):
                load_bc(0, n, n, True)
            load_rows(0, True)
            load_expert(0, 0, 0, True)
            load_expert(0, 1, 1, True)
            for n in range(2, 4):
                load_bc(0, n, n % 2, False)
            with sync.Fori(1, 4) as g:
                for n in range(4):
                    load_bc(0, 4 * g + n, n % 2, False)
            with sync.Fori(1, NB) as c:
                for n in range(2):
                    load_bc(c, n, n, False)
                load_gnn(c - 1)
                for n in range(2, 4):
                    load_bc(c, n, n % 2, False)
                with sync.Fori(1, 4) as g:
                    for n in range(4):
                        load_bc(c, 4 * g + n, n % 2, False)
                        if n in (1, 3):
                            load_expert(c - 1, 2 * g + n // 2, n // 2, False)
                store(c - 1)
                load_rows(c, False)
                for e in range(2):
                    load_expert(c, e, e, False)
            load_gnn(NB - 1)
            with sync.Fori(1, 4) as g:
                for e in range(2):
                    load_expert(NB - 1, 2 * g + e, e, False)
            store(NB - 1)
            await_ge(sync, out_saved, 16 * NB)

        @block.gpsimd
        def _(pool):
            pool.memset(ident[:, :], 0.0).then_inc(pool_made, 1)
            pool.wait_ge(pool_made, 1)
            pool.affine_select(out=ident[:, :], in_=ident[:, :], compare_op=ALU.not_equal, fill=1.0,
                               base=0, pattern=[[-1, P]], channel_multiplier=1).then_inc(pool_made, 1)
            pool.memset(ones, 1.0).then_inc(pool_made, 1)
            pool.memset(eps_c[:, :], EPS).then_inc(pool_made, 1)
            pool.memset(guard_c[:, :], -0.5 * math.log(SCAN_EPS)).then_inc(pool_made, 1)
            pool.memset(carry[:, :, :], 0.0).then_inc(pool_made, 1)
            pool.wait_ge(pool_made, 6)
            pool.nop().then_inc(phase_a, 1)

            def b_times(c, n, s, hf, first):
                pair = NP_CHUNK * c + 2 * n + hf
                if hf == 0:
                    await_ge(pool, bc_loaded[s], 16 * (c * (NS // 2) + (n - s) // 2 + 1))
                if not first:
                    await_ge(pool, scanned, 2 * (pair - 1))
                pool.tensor_tensor(bu[:, hf, :, :],
                                   arena[:, c, S0 + 2 * hf:S0 + 2 * hf + 2, :],
                                   bc[:, s, 0:1, :].broadcast_to([P, 2, BLK]), ALU.mult)\
                    .then_inc(bu_made, 1)

            def add_up(c, n, hf):
                pair = NP_CHUNK * c + 2 * n + hf
                await_ge(pool, weighted, pair + 1)
                y = arena[:, c, U0 + 2 * hf:U0 + 2 * hf + 2, :]
                pool.tensor_tensor(y, y, yc[:, hf, :, :], ALU.add).then_inc(summed, 1)

            def group(c, g, first):
                for n in range(4):
                    for hf in range(2):
                        b_times(c, 4 * g + n, n % 2, hf, first and n == 0)
                        if not (first and n == 0):
                            if n:
                                add_up(c, 4 * g + n - 1, hf)
                            else:
                                add_up_last(c, g, hf)

            def add_up_last(c, g, hf):
                add_up(c, 4 * g - 1, hf)

            pool.wait_ge(phase_a, 4)
            await_ge(pool, delta_made, CI * NB)
            await_ge(pool, skip_made, NB)

            def chunk(c, first):
                for n in range(4):
                    for hf in range(2):
                        b_times(c, n, n % 2, hf, first and n == 0)
                        if n:
                            add_up(c, n - 1, hf)
                with pool.Fori(1, 4) as g:
                    for n in range(4):
                        for hf in range(2):
                            b_times(c, 4 * g + n, n % 2, hf, False)
                            add_up(c, 4 * g + n - 1, hf)
                for hf in range(2):
                    add_up(c, NS - 1, hf)

            chunk(0, True)
            with pool.Fori(1, NB) as c:
                chunk(c, False)

        @block.tensor
        def _(pe):
            pe.wait_ge(pool_made, 2)
            pe.wait_ge(consts_loaded, 16 * CONSTS)
            for a in range(CD):
                for c in range(CD):
                    ins = pe.transpose(ps[:, 0, (c * CD + a) * P:(c * CD + a + 1) * P],
                                       wnat[:, a, c * P:(c + 1) * P], ident[:, :])
            ins = pe.transpose(ps[:, 1, 0:VECS], vec_rows[:, :], ident[0:VECS, 0:VECS])
            ins.then_inc(w_turned, 1)
            pe.wait_ge(w_kept, 2)

            def turn_rows(t, s, first):
                pe.wait_ge(diag_added, t + 1)
                for b in range(4):
                    if not first:
                        pe.wait_ge(adj_kept, 4 * (t - 2) + b + 1)
                    for j in range(4):
                        ins = pe.transpose(ps[:, 4 * (s % 2) + b, j * P:(j + 1) * P],
                                           ring[:, s, (4 * b + j) * P:(4 * b + j + 1) * P], ident[:, :])
                    ins.then_inc(adj_turned, 1)

            for s in range(4):
                turn_rows(s, s, s < 2)
            with pe.Fori(1, NT // 4) as it:
                for s in range(4):
                    turn_rows(4 * it + s, s, False)

            S_, W_, T_, I_ = 0, 2, 4, 6

            def gcn(k, c):
                for j in range(NT):
                    ins = pe.matmul(ps[:, S_ + c, :], z[:, j, c * P:(c + 1) * P], arena[:, k, j, :],
                                    start=(j == 0), stop=(j == NT - 1))
                ins.then_inc(gcn_done, 1)

            pe.wait_ge(adj_kept, 4 * NT)
            pe.wait_ge(z_made, NT)
            gcn(0, 0)
            gcn(0, 1)

            def block_a(k, first, last):
                pe.wait_ge(gT_kept, 2 * (k + 1))
                for t in range(TB):
                    for c in range(CD):
                        ins = pe.matmul(ps[:, W_ + t // 2, (t % 2) * D:(t % 2 + 1) * D],
                                        gT[:, c, t * P:(t + 1) * P], wT[:, c, :],
                                        start=(c == 0 and t % 2 == 0), stop=(c == CD - 1),
                                        skip_group_check=True)
                    ins.then_inc(wmm_done, 1)
                if not last:
                    gcn(k + 1, 0)
                for t in range(TB):
                    pe.wait_ge(pre_made, TB * k + t + 1)
                    if t == 0 and not first:
                        pe.wait_ge(dt_relu, CI * k)
                    for c in range(CD):
                        ins = pe.transpose(ps[:, T_ + c, t * P:(t + 1) * P],
                                           pre[:, t, c * P:(c + 1) * P], ident[:, :])
                ins.then_inc(pre_turned, 1)
                pe.wait_ge(preT_kept, 2 * (k + 1))
                for m in range(2 * CI):
                    if m >= 2:
                        pe.wait_ge(inproj_used, 2 * CI * k + m - 1)
                    elif not first:
                        pe.wait_ge(dt_relu, CI * k)
                    for c in range(CD):
                        ins = pe.matmul(ps[:, I_ + m % 2, :], win_sb[:, c, m * P:(m + 1) * P],
                                        preT[:, c, :], start=(c == 0), stop=(c == CD - 1))
                    ins.then_inc(inproj_done, 1)
                if not last:
                    gcn(k + 1, 1)
                for c in range(CI):
                    pe.wait_ge(u_made, CI * k + c + 1)
                    ins = pe.matmul(ps[0:XD, W_, :], wx_sb[:, c, :], arena[:, k, U0 + c, :],
                                    start=(c == 0), stop=(c == CI - 1))
                ins.then_inc(xdbl_done, 1)
                pe.wait_ge(xdbl_kept, k + 1)
                for m in range(CI):
                    pe.matmul(ps[:, T_ + m, :], wdt_sb[0:DTR, m * P:(m + 1) * P], xdbl[0:DTR, :],
                              start=True, stop=True).then_inc(dt_done, 1)

            block_a(0, True, False)
            with pe.Fori(1, NB - 1) as k:
                block_a(k, False, False)
            block_a(NB - 1, False, True)
            pe.wait_ge(dt_done, CI * NB)
            pe.nop().then_inc(phase_a, 1)
            pe.wait_ge(phase_a, 4)

            O_, M_ = 4, 6

            def prep(c, first):
                pe.wait_ge(yg_made, c + 1)
                for t in range(TB):
                    for m in range(CI):
                        ins = pe.matmul(ps[:, O_ + t // 2, (t % 2) * D:(t % 2 + 1) * D],
                                        hT[:, m, t * P:(t + 1) * P], wout_sb[:, m, :],
                                        start=(m == 0 and t % 2 == 0), stop=(m == CI - 1),
                                        skip_group_check=True)
                ins.then_inc(mamba_done, 1)
                for t in range(TB):
                    pe.wait_ge(xm_made, TB * c + t + 1)
                    for a in range(CD):
                        ins = pe.transpose(ps[:, M_ + a, t * P:(t + 1) * P],
                                           xm[:, t, a * P:(a + 1) * P], ident[:, :])
                ins.then_inc(xm_turned, 1)
                pe.wait_ge(xmT_kept, 2 * (c + 1))
                for t in range(TB):
                    for a in range(CD):
                        ins = pe.matmul(ps[:, O_, t * NE:(t + 1) * NE], xmT[:, a, t * P:(t + 1) * P],
                                        wg_sb[:, a, :], start=(a == 0 and t == 0), stop=(a == CD - 1),
                                        skip_group_check=True)
                ins.then_inc(gate_done, 1)
                pe.wait_ge(gw_made, c + 1)
                for t in range(TB):
                    ins = pe.transpose(ps[0:NE, O_ + 1, t * P:(t + 1) * P], gw[:, t, :], ident[:, :])
                ins.then_inc(gw_turned, 1)
                pe.wait_ge(gateT_kept, c + 1)
                for t in range(TB):
                    ins = pe.matmul(ps[:, O_ + t // 2, (t % 2) * D:(t % 2 + 1) * D],
                                    gateT[0:NE, t * P:(t + 1) * P], b2_sb[:, :],
                                    start=(t % 2 == 0), stop=True, skip_group_check=True)
                ins.then_inc(b2_done, 1)
                pe.wait_ge(b2_used, c + 1)

            def expert(c, e, s, first_of_chunk):
                count = NE * c + e
                pe.wait_ge(wt_loaded[s], 32 * (c * (NE // 2) + (e - s) // 2 + 1))
                for m in range(CI):
                    if m >= 2 or not first_of_chunk:
                        pe.wait_ge(hid_kept, CI * count + m - 1)
                    for a in range(CD):
                        ins = pe.matmul(ps[:, M_ + m % 2, :],
                                        w1_sb[:, s, a * DI + m * P:a * DI + (m + 1) * P],
                                        xmT[:, a, :], start=(a == 0), stop=(a == CD - 1))
                    ins.then_inc(hid_done, 1)
                pe.wait_ge(hid_kept, CI * (count + 1))
                for t in range(TB):
                    if t % 2 == 0 and not first_of_chunk:
                        pe.wait_ge(exp_used, TB * (count - 1) + t + 2)
                    for m in range(CI):
                        ins = pe.matmul(ps[:, O_ + t // 2, (t % 2) * D:(t % 2 + 1) * D],
                                        hT[:, m, t * P:(t + 1) * P], w2_sb[:, s, m * D:(m + 1) * D],
                                        start=(m == 0 and t % 2 == 0), stop=(m == CI - 1),
                                        skip_group_check=True)
                    ins.then_inc(exp_done, 1)

            prep(0, True)
            with pe.Fori(0, NB - 1) as c:
                for e in range(2):
                    expert(c, e, e, e == 0)
                with pe.Fori(1, 4) as g:
                    for e in range(2):
                        expert(c, 2 * g + e, e, False)
                prep(c + 1, False)
            for e in range(2):
                expert(NB - 1, e, e, e == 0)
            with pe.Fori(1, 4) as g:
                for e in range(2):
                    expert(NB - 1, 2 * g + e, e, False)

        @block.scalar
        def _(act):
            act.wait_ge(w_turned, 1)
            act.activation(wT, ps[:, 0, :].rearrange("p (a n) -> p a n", a=CD), ACT.Copy)\
                .then_inc(w_kept, 1)
            act.activation(vecs[:, :], ps[:, 1, 0:VECS], ACT.Copy).then_inc(w_kept, 1)

            def keep_rows(t, s):
                blk = (t - s) // 4 if isinstance(t, int) else t_block
                for b in range(4):
                    await_ge(act, adj_turned, 4 * t + b + 1)
                    act.activation(arena[:, blk, 4 * b:4 * b + 4, s * P:(s + 1) * P],
                                   ps[:, 4 * (s % 2) + b, :].rearrange("p (j i) -> p j i", j=4),
                                   ACT.Copy).then_inc(adj_kept, 1)

            t_block = 0
            for s in range(4):
                keep_rows(s, s)
            with act.Fori(1, NT // 4) as it:
                t_block = it
                for s in range(4):
                    keep_rows(4 * it + s, s)

            await_ge(act, row_summed, NT)
            act.wait_ge(pool_made, 6)
            act.activation(sa[:, :], rowsum[:, :], ACT.Sqrt).then_inc(roots_a, 1)
            act.wait_ge(dve_a, 1)
            act.activation(sb_[:, :], mv[:, :, 1], ACT.Sqrt, bias=eps_c[:, :]).then_inc(roots_a, 1)
            await_ge(act, consts_loaded, 16 * CONSTS)
            act.activation(amat[:, :, :], amat[:, :, :], ACT.Exp).then_inc(act_a, 1)
            act.wait_ge(act_a, 1)
            act.activation(ahalf[:, :, :], amat[:, :, :], ACT.Copy, scale=-0.5).then_inc(act_a, 1)
            act.wait_ge(act_a, 2)
            act.activation(amat[:, :, :], amat[:, :, :], ACT.Copy, scale=-1.0).then_inc(act_a, 1)

            S_, W_, T_, I_ = 0, 2, 4, 6

            def block_a(k, first):
                await_ge(act, gcn_done, 2 * k + 1)
                if not first:
                    await_ge(act, wmm_done, TB * k)
                act.activation(gT[:, 0, :], ps[:, S_, :], ACT.Copy).then_inc(gT_kept, 1)
                await_ge(act, q_made, k + 1)
                act.activation(qr[:, :], q[:, :], ACT.Sqrt).then_inc(q_rooted, 1)
                await_ge(act, pre_turned, k + 1)
                act.activation(preT[:, 0, :], ps[:, T_, :], ACT.Copy, scale=w1c[:, 0:1])\
                    .then_inc(preT_kept, 1)
                for m in range(CI):
                    await_ge(act, inproj_done, 2 * CI * k + m + 1)
                    if m == 0 and not first:
                        await_ge(act, conv_done, (CI + 1) * k + 1)
                    act.activation(stage[:, m, 3:3 + BLK], ps[:, I_ + m % 2, :], ACT.Copy)\
                        .then_inc(inproj_used, 1)
                for m in range(CI):
                    await_ge(act, inproj_done, 2 * CI * k + CI + m + 1)
                    act.activation(arena[:, k, G0 + m, :], ps[:, I_ + m % 2, :], ACT.Silu)\
                        .then_inc(inproj_used, 1)
                for m in range(CI):
                    await_ge(act, conv_done, (CI + 1) * k + m + 2)
                    act.activation(arena[:, k, U0 + m, :], arena[:, k, U0 + m, :], ACT.Silu,
                                   bias=cb[:, m:m + 1]).then_inc(u_made, 1)
                await_ge(act, xdbl_done, k + 1)
                if not first:
                    await_ge(act, bc_saved, 16 * k)
                act.activation(xdbl[0:XD, :], ps[0:XD, W_, :], ACT.Copy).then_inc(xdbl_kept, 1)
                for m in range(CI):
                    await_ge(act, dt_done, CI * k + m + 1)
                    act.activation(arena[:, k, D0 + m, :], ps[:, T_ + m, :], ACT.Abs,
                                   bias=bdt[:, m:m + 1]).then_inc(dt_abs, 1)
                dl = arena[:, k, D0:D0 + CI, :]
                await_ge(act, dt_abs, CI * (k + 1))
                act.activation(dl, dl, ACT.Exp, scale=-1.0).then_inc(act_soft, 1)
                await_ge(act, act_soft, k + 1)
                act.activation(dl, dl, ACT.Ln, bias=1.0).then_inc(soft_made, 1)

            block_a(0, True)
            with act.Fori(1, NB) as k:
                block_a(k, False)
            await_ge(act, soft_made, NB)
            act.activation(gmax[:, 0:1], eps_c[:, :], ACT.Exp).then_inc(phase_a, 1)
            act.wait_ge(phase_a, 4)
            act.wait_ge(act_a, 3)

            def decay(c, n, s, hf, first):
                pair = NP_CHUNK * c + 2 * n + hf
                if not first:
                    await_ge(act, weighted, pair - 1)
                for j in range(2):
                    m = 2 * hf + j
                    act.activation(ps[:, m, :], arena[:, c, D0 + m, :], ACT.Exp,
                                   scale=amat[:, m, bass.ds(n, 1)]).then_inc(a_made, 1)
                for j in range(2):
                    m = 2 * hf + j
                    act.activation(gate[:, hf, j, :], rsum[:, m, :], ACT.Tanh,
                                   scale=ahalf[:, m, bass.ds(n, 1)], bias=guard_c[:, :])\
                        .then_inc(gate_made, 1)

            def group(c, g, first, experts):
                for n in range(4):
                    for hf in range(2):
                        decay(c, 4 * g + n, n % 2, hf, first and n == 0)
                    if experts and n % 2 == 1:
                        hidden(c - 1, 2 * g + n // 2)

            def hidden(c, e):
                count = NE * c + e
                for m in range(CI):
                    await_ge(act, hid_done, CI * count + m + 1)
                    if m == 0 and not (isinstance(e, int) and e == 0):
                        await_ge(act, exp_done, TB * count)
                    act.activation(hT[:, m, :], ps[:, 6 + m % 2, :], ACT.Silu,
                                   bias=vecs[:, bass.ds(B1 + CI * e + m, 1)]).then_inc(hid_kept, 1)

            def prep(c):
                await_ge(act, v_made, c + 1)
                for t in range(TB):
                    act.activation(xm[:, t, :], acc[:, t, :], ACT.Square, accum_out=ss[:, t:t + 1])\
                        .then_inc(ss_made, 1)
                await_ge(act, ss_made, TB * (c + 1))
                act.activation(r2[:, :], ss[:, :], ACT.Sqrt, scale=1.0 / D, bias=eps_c[:, :])\
                    .then_inc(ss_rooted, 1)
                await_ge(act, xm_turned, c + 1)
                act.activation(xmT[:, 0, :], ps[:, 6, :], ACT.Copy, scale=w2c[:, 0:1])\
                    .then_inc(xmT_kept, 1)
                await_ge(act, logit_made, c + 1)
                act.activation(gw[:, :, :], gw[:, :, :], ACT.Exp).then_inc(gexp_made, 1)
                await_ge(act, gw_turned, c + 1)
                act.activation(gateT[0:NE, :], ps[0:NE, 5, :], ACT.Copy).then_inc(gateT_kept, 1)

            act.wait_ge(r_made, 1)
            group(0, 0, True, False)
            with act.Fori(1, 4) as g:
                group(0, g, False, False)
            prep(0)
            with act.Fori(1, NB) as c:
                await_ge(act, r_made, c + 1)
                group(c, 0, False, True)
                with act.Fori(1, 4) as g:
                    group(c, g, False, True)
                prep(c)
            hidden(NB - 1, 0)
            with act.Fori(1, NE) as e:
                hidden(NB - 1, e)

        @block.vector
        def _(dve):
            dve.wait_ge(x_loaded, 16)
            for t in range(NT):
                dve.bn_stats(stats[:, t, :], xrow[:, t, :]).then_inc(dve_r, 1)
            await_ge(dve, dve_r, NT)
            for t in range(NT):
                ins = dve.bn_aggr(mv[:, t, :], stats[:, t, :])
            ins.then_inc(dve_a, 1)
            dve.wait_ge(pool_made, 2)

            def sum_rows(t, s, loaded):
                await_ge(dve, adj_loaded[s], 16 * loaded)
                d = ring[:, s, bass.ds(t * P, P)]
                dve.tensor_tensor(d, d, ident[:, :], ALU.add).then_inc(diag_added, 1)
                await_ge(dve, diag_added, t + 1)
                dve.tensor_reduce(rowsum[:, bass.ds(t, 1)], ring[:, s, :], AX, ALU.add)\
                    .then_inc(row_summed, 1)

            for s in range(4):
                sum_rows(s, s, 1)
            with dve.Fori(1, NT // 4) as it:
                for s in range(4):
                    sum_rows(4 * it + s, s, it + 1)

            a = Steps(dve, dve_a, 0)
            a.n = 1

            def newton(st, y, v, tmp):
                st.did(dve.tensor_tensor(tmp, y, y, ALU.mult))
                st.wait()
                st.did(dve.tensor_tensor(tmp, tmp, v, ALU.mult))
                st.wait()
                st.did(dve.tensor_scalar(tmp, tmp, -0.5, 1.5, ALU.mult, ALU.add))
                st.wait()
                st.did(dve.tensor_tensor(y, y, tmp, ALU.mult))
                st.wait()

            dve.wait_ge(roots_a, 2)
            await_ge(dve, row_summed, NT)
            a.did(dve.reciprocal(deg[:, :], sa[:, :]))
            a.did(dve.reciprocal(zscale[:, :], sb_[:, :]))
            a.did(dve.tensor_scalar(sd_[:, :], mv[:, :, 1], EPS, None, ALU.add))
            a.wait()
            newton(a, deg[:, :], rowsum[:, :], sc_[:, :])
            newton(a, zscale[:, :], sd_[:, :], sc_[:, :])
            a.did(dve.tensor_tensor(zscale[:, :], zscale[:, :], deg[:, :], ALU.mult))
            a.wait()
            for t in range(NT):
                dve.tensor_scalar(z[:, t, :], xrow[:, t, :], mv[:, t, 0:1], zscale[:, t:t + 1],
                                  ALU.subtract, ALU.mult).then_inc(z_made, 1)
            dve.memset(stage[:, :, 0:3], 0.0).then_inc(conv_done, 1)

            S_, W_, T_, I_ = 0, 2, 4, 6
            PER_A = 4 * TB + 1 + 1 + 4 + 2 + 12 + 4 + 1 + 100

            def block_a(k, first):
                st = Steps(dve, dve_b, k * STEPS_A)
                await_ge(dve, gcn_done, 2 * k + 2)
                if not first:
                    await_ge(dve, wmm_done, TB * k)
                dve.tensor_copy(gT[:, 1, :], ps[:, S_ + 1, :]).then_inc(gT_kept, 1)
                if not first:
                    await_ge(dve, rows_saved, 32 * k)
                xb = xrow_block(k)
                for t in range(TB):
                    await_ge(dve, wmm_done, TB * k + 2 * (t // 2) + 2)
                    st.did(dve.scalar_tensor_tensor(
                        normed[:, t, :], ps[:, W_ + t // 2, (t % 2) * D:(t % 2 + 1) * D],
                        deg[:, bass.ds(TB * k + t, 1)], gb_bc, ALU.mult, ALU.add))
                for t in range(TB):
                    st.wait(TB - 1)
                    st.did(dve.scalar_tensor_tensor(
                        xb[:, t, :], normed[:, t, :], 0.0, xb[:, t, :], ALU.max, ALU.add))
                for t in range(TB):
                    st.wait(TB - 1)
                    st.did(dve.bn_stats(stats2[:, t, :], xb[:, t, :]))
                for t in range(TB):
                    st.wait(TB - 1)
                    st.did(dve.bn_aggr(mv2[:, t, :], stats2[:, t, :]))
                st.wait()
                st.did(dve.tensor_scalar(q[:, 0:TB], mv2[:, :, 1], EPS, None, ALU.add))
                st.wait()
                dve.scalar_tensor_tensor(q[:, TB:], q[:, 0:TB], EPS, mv2[:, :, 1], ALU.mult, ALU.add)\
                    .then_inc(q_made, 1)
                await_ge(dve, q_made, k + 1)
                dve.nop().then_inc(x1_made, 1)
                await_ge(dve, q_rooted, k + 1)
                st.did(dve.reciprocal(qr[:, :], qr[:, :]))
                st.wait()
                newton(st, qr[:, :], q[:, :], qt[:, :])
                for t in range(TB):
                    dve.tensor_scalar(pre[:, t, :], xb[:, t, :], mv2[:, t, 0:1],
                                      qr[:, TB + t:TB + t + 1], ALU.subtract, ALU.mult)
                    dve.tensor_scalar(normed[:, t, :], xb[:, t, :], mv2[:, t, 0:1], qr[:, t:t + 1],
                                      ALU.subtract, ALU.mult).then_inc(pre_made, 1)
                await_ge(dve, pre_turned, k + 1)
                dve.tensor_scalar(preT[:, 1, :], ps[:, T_ + 1, :], w1c[:, 1:2], None, ALU.mult)\
                    .then_inc(preT_kept, 1)
                for m in range(CI):
                    await_ge(dve, inproj_used, 2 * CI * k + m + 1)
                    o = arena[:, k, U0 + m, :]
                    st.did(dve.tensor_scalar(o, stage[:, m, 0:BLK], cw[:, m, 0:1], None, ALU.mult))
                    for j in range(1, 4):
                        st.wait()
                        ins = dve.scalar_tensor_tensor(o, stage[:, m, j:j + BLK], cw[:, m, j:j + 1],
                                                       o, ALU.mult, ALU.add)
                        if j < 3:
                            st.did(ins)
                        else:
                            ins.then_inc(conv_done, 1)
                await_ge(dve, conv_done, (CI + 1) * k + CI + 1)
                dve.tensor_copy(stage[:, :, 0:3], stage[:, :, BLK:BLK + 3]).then_inc(conv_done, 1)
                for m in range(CI):
                    await_ge(dve, dt_done, CI * k + m + 1)
                    await_ge(dve, dt_abs, CI * k + m + 1)
                    dve.tensor_scalar(arena[:, k, S0 + m, :], ps[:, T_ + m, :], bdt[:, m:m + 1], 0.0,
                                      ALU.add, ALU.max).then_inc(dt_relu, 1)
                await_ge(dve, soft_made, k + 1)
                await_ge(dve, dt_relu, CI * (k + 1))
                for m in range(CI):
                    d = arena[:, k, D0 + m, :]
                    st.did(dve.scalar_tensor_tensor(d, arena[:, k, S0 + m, :], 1.0, d, ALU.mult,
                                                    ALU.add, accum_out=tot[:, m, bass.ds(k, 1)]))
                for m in range(CI):
                    st.wait(CI - 1)
                    st.did(dve.scalar_tensor_tensor(arena[:, k, S0 + m, :], arena[:, k, D0 + m, :],
                                                    0.5, arena[:, k, U0 + m, :], ALU.mult, ALU.mult))
                await_ge(dve, xdbl_done, k + 1)
                for m in range(CI):
                    st.wait(CI - 1)
                    u = arena[:, k, U0 + m, :]
                    st.did(dve.tensor_scalar(u, u, dp[:, m:m + 1], None, ALU.mult))
                st.wait()
                dve.nop().then_inc(skip_made, 1)
                return st.n

            STEPS_A = 4 * TB + 1 + 1 + 4 + 3 * CI + 3 * CI
            assert block_a(0, True) == STEPS_A
            with dve.Fori(1, NB) as k:
                block_a(k, False)
            st = Steps(dve, dve_b, NB * STEPS_A)
            st.did(dve.memset(suffix[:, :, NB - 1], 0.0))
            for k in range(NB - 2, -1, -1):
                st.wait()
                st.did(dve.tensor_tensor(suffix[:, :, k], suffix[:, :, k + 1], tot[:, :, k + 1],
                                         ALU.add))
            st.wait()
            dve.nop().then_inc(delta_made, CI * NB)
            dve.nop().then_inc(phase_a, 1)
            dve.wait_ge(phase_a, 4)

            def make_r(c):
                dve.tensor_copy(gate_all, arena[:, c, D0:D0 + CI, :]).then_inc(dve_c, 1)
                dve.tensor_copy(rsum[:, :, BLK - 1:BLK], suffix[:, :, bass.ds(c, 1)])
                await_ge(dve, dve_c, c + 1)
                for m in range(CI):
                    ins = dve.tensor_tensor_scan(
                        rsum[:, m, 0:BLK - 1][:, ::-1], ones[:, 0:BLK - 1],
                        gate_all[:, m, 1:BLK][:, ::-1], suffix[:, m, bass.ds(c, 1)],
                        ALU.mult, ALU.add)
                ins.then_inc(r_made, 1)

            def scans(c, n, hf, first_chunk):
                pair = NP_CHUNK * c + 2 * n + hf
                await_ge(dve, bu_made, pair + 1)
                if not first_chunk and hf == 0:
                    await_ge(dve, carried, NP_CHUNK * (c - 1) + 2 * n + 2)
                for j in range(2):
                    m = 2 * hf + j
                    await_ge(dve, a_made, 2 * pair + j + 1)
                    dve.tensor_tensor_scan(ps[:, m, :], ps[:, m, :], bu[:, hf, j, :],
                                           carry[:, m, bass.ds(n, 1)], ALU.mult, ALU.add)\
                        .then_inc(scanned, 1)

            def guard(c, n, hf):
                pair = NP_CHUNK * c + 2 * n + hf
                h = ps[:, 2 * hf:2 * hf + 2, :]
                await_ge(dve, scanned, 2 * pair + 2)
                dve.tensor_copy(carry[:, 2 * hf:2 * hf + 2, bass.ds(n, 1)],
                                ps[:, 2 * hf:2 * hf + 2, BLK - 1:BLK]).then_inc(carried, 1)
                await_ge(dve, gate_made, 2 * pair + 2)
                await_ge(dve, carried, pair + 1)
                dve.scalar_tensor_tensor(h, gate[:, hf, :, :], 1.0, h, ALU.add, ALU.mult)\
                    .then_inc(guarded, 1)

            def weigh(c, n, s, hf, first):
                pair = NP_CHUNK * c + 2 * n + hf
                await_ge(dve, guarded, pair + 1)
                if not first:
                    await_ge(dve, summed, pair - 1)
                dve.tensor_tensor(yc[:, hf, :, :], ps[:, 2 * hf:2 * hf + 2, :],
                                  bc[:, s, 1:2, :].broadcast_to([P, 2, BLK]), ALU.mult)\
                    .then_inc(weighted, 1)

            def state(c, n, s, first, first_chunk):
                await_ge(dve, bc_loaded[s], 16 * (c * (NS // 2) + (n - s) // 2 + 1))
                scans(c, n, 0, first_chunk)
                guard(c, n, 0)
                weigh(c, n, s, 0, first)
                scans(c, n, 1, first_chunk)
                guard(c, n, 1)
                weigh(c, n, s, 1, first)

            def prep(c):
                st = Steps(dve, dve_p, c * STEPS_P)
                await_ge(dve, summed, NP_CHUNK * (c + 1))
                dve.tensor_tensor(hT, arena[:, c, U0:U0 + CI, :], arena[:, c, G0:G0 + CI, :], ALU.mult)\
                    .then_inc(yg_made, 1)
                await_ge(dve, normed_loaded, 16 * (c + 1))
                await_ge(dve, mamba_done, c + 1)
                o = ps[:, 4:6, :].rearrange("p a (b d) -> p (a b) d", b=2)
                dve.tensor_tensor(acc, o, acc, ALU.add).then_inc(v_made, 1)
                await_ge(dve, ss_made, TB * (c + 1))
                st.did(dve.tensor_scalar(ssv[:, :], ss[:, :], 1.0 / D, EPS, ALU.mult, ALU.add))
                await_ge(dve, ss_rooted, c + 1)
                st.did(dve.reciprocal(r2[:, :], r2[:, :]))
                st.wait()
                newton(st, r2[:, :], ssv[:, :], r2t[:, :])
                await_ge(dve, v_made, c + 1)
                for t in range(TB):
                    dve.tensor_scalar(xm[:, t, :], acc[:, t, :], r2[:, t:t + 1], None, ALU.mult)\
                        .then_inc(xm_made, 1)
                await_ge(dve, xm_turned, c + 1)
                dve.tensor_scalar(xmT[:, 1, :], ps[:, 7, :], w2c[:, 1:2], None, ALU.mult)\
                    .then_inc(xmT_kept, 1)
                await_ge(dve, gate_done, c + 1)
                lg = ps[:, 4, 0:TB * NE].rearrange("p (t e) -> p t e", t=TB)
                st.did(dve.tensor_reduce(gmax[:, :], lg, AX, ALU.max))
                st.wait()
                dve.tensor_tensor(gw[:, :, :], lg, gmax[:, :].unsqueeze(2).broadcast_to([P, TB, NE]),
                                  ALU.subtract).then_inc(logit_made, 1)
                await_ge(dve, gexp_made, c + 1)
                st.did(dve.tensor_reduce(gsum[:, :], gw[:, :, :], AX, ALU.add))
                st.wait()
                st.did(dve.reciprocal(gsum[:, :], gsum[:, :]))
                st.wait()
                dve.tensor_tensor(gw[:, :, :], gw[:, :, :],
                                  gsum[:, :].unsqueeze(2).broadcast_to([P, TB, NE]), ALU.mult)\
                    .then_inc(gw_made, 1)
                await_ge(dve, b2_done, c + 1)
                st.did(dve.tensor_tensor(acc, o, acc, ALU.add))
                await_ge(dve, gnn_loaded, 16 * (c + 1))
                st.wait()
                dve.tensor_tensor(acc, acc, xm, ALU.add).then_inc(b2_used, 1)
                return st.n

            def mix(c, e, last):
                count = NE * c + e
                for t in range(TB):
                    await_ge(dve, exp_done, TB * count + t + 1 if t % 2 else TB * count + t + 2)
                    if not isinstance(e, int) or e > 0:
                        await_ge(dve, exp_used, TB * (count - 1) + t + 1)
                    elif t == 0:
                        await_ge(dve, b2_used, c + 1)
                    dve.scalar_tensor_tensor(acc[:, t, :],
                                             ps[:, 4 + t // 2, (t % 2) * D:(t % 2 + 1) * D],
                                             gw[:, t, bass.ds(e, 1)], acc[:, t, :],
                                             ALU.mult, ALU.add).then_inc(exp_used, 1)

            def group(c, g, first, first_chunk, experts):
                for n in range(4):
                    state(c, 4 * g + n, n % 2, first and n == 0, first_chunk)
                    if experts and n % 2 == 1:
                        mix(c - 1, 2 * g + n // 2, False)

            STEPS_P = 6 + 1 + 2 + 1
            make_r(0)
            group(0, 0, True, True, False)
            with dve.Fori(1, 4) as g:
                group(0, g, False, True, False)
            make_r(1)
            assert prep(0) == STEPS_P
            with dve.Fori(1, NB - 1) as c:
                group(c, 0, False, False, True)
                with dve.Fori(1, 4) as g:
                    group(c, g, False, False, True)
                await_ge(dve, exp_used, TB * NE * c)
                dve.nop().then_inc(acc_done, 1)
                make_r(c + 1)
                prep(c)
            c = NB - 1
            group(c, 0, False, False, True)
            with dve.Fori(1, 4) as g:
                group(c, g, False, False, True)
            await_ge(dve, exp_used, TB * NE * c)
            dve.nop().then_inc(acc_done, 1)
            prep(c)
            mix(c, 0, False)
            with dve.Fori(1, NE) as e:
                mix(c, e, False)
            await_ge(dve, exp_used, TB * NE * NB)
            dve.nop().then_inc(acc_done, 1)


_INS = ['x', 'adj', 'L0_gnn_W', 'L0_gnn_b', 'L0_ffn_w_rms1', 'L0_ffn_w_rms2', 'L0_ffn_W_in',
        'L0_ffn_conv_w', 'L0_ffn_conv_b', 'L0_ffn_W_x', 'L0_ffn_W_dt', 'L0_ffn_b_dt', 'L0_ffn_A_log',
        'L0_ffn_Dp', 'L0_ffn_W_out', 'L0_ffn_W_gate', 'L0_ffn_W1', 'L0_ffn_b1', 'L0_ffn_W2',
        'L0_ffn_b2']


def kernel(**inputs):
    import numpy as np
    import concourse.bacc as bacc
    from concourse.bass_utils import run_bass_kernel_spmd

    nc = bacc.Bacc("TRN2", target_bir_lowering=False, num_devices=1, dynamic_dma_scratch_size=1024)
    arrays, args = {}, []
    for name in _INS:
        a = np.ascontiguousarray(inputs[name])
        arrays[f"in_{name}"] = a
        args.append(nc.dram_tensor(f"in_{name}", a.shape, mybir.dt.from_np(a.dtype),
                                   kind="ExternalInput").ap())
    out = nc.dram_tensor("out_rows", inputs['x'].shape, F32, kind="ExternalOutput").ap()
    build(nc, *args, out)
    r = run_bass_kernel_spmd(nc, [arrays], core_ids=[0])
    return r.results[0]["out_rows"]
```

```python
import math
from contextlib import ExitStack

import concourse.bass as bass
from concourse import mybir

F32 = mybir.dt.float32
ALU = mybir.AluOpType
ACT = mybir.ActivationFunctionType
AX = mybir.AxisListType.X

P = 128
BLK = 512
EPS = 1e-5
SCAN_EPS = 1e-12


def await_ge(eng, sem, value):
    eng.wait_ge(sem, value)
    if not isinstance(value, int):
        eng.nop(nofuse=True)


class Steps:

    def __init__(self, eng, sem, start):
        self.eng, self.sem, self.n, self.start = eng, sem, 0, start

    def did(self, ins):
        ins.then_inc(self.sem, 1)
        self.n += 1

    def wait(self, back=0):
        await_ge(self.eng, self.sem, self.start + (self.n - back))


def build(nc, x, adj, gnn_w, gnn_b, w_rms1, w_rms2, w_in, conv_w, conv_b, w_x, w_dt, b_dt, a_log,
          d_skip, w_out, w_gate, w1, b1, w2, b2, out):
    L, D = x.shape
    DI = w_out.shape[0]
    NS = a_log.shape[1]
    DTR = w_dt.shape[0]
    NE = w_gate.shape[1]
    NT = L // P
    NB = L // BLK
    TB = BLK // P
    CD = D // P
    CI = DI // P
    XD = DTR + 2 * NS
    assert (CD, CI, TB, NB, NS, NE, XD) == (2, 4, 4, 4, 16, 8, 64)

    gnn_rows = nc.dram_tensor("gnn_rows", [L, D], F32, kind="Internal").ap()
    norm_rows = nc.dram_tensor("norm_rows", [L, D], F32, kind="Internal").ap()
    bc_rows = nc.dram_tensor("bc_rows", [2 * NS, L], F32, kind="Internal").ap()
    bc_pairs = bc_rows.rearrange("(a n) l -> n a l", a=2)
    adj_t = adj.rearrange("(t p) j -> t p j", p=P)

    ctx = ExitStack()
    with ctx:
        def sb(name, shape):
            return ctx.enter_context(nc.sbuf_tensor(name, shape, F32))

        def sem(name):
            return ctx.enter_context(nc.semaphore(name))

        arena = sb("arena", [P, NB, NT, BLK])
        U0, G0, D0, S0 = 0, CI, 2 * CI, 3 * CI
        low = sb("low", [P, 23040])

        def view(at, *dims):
            n = math.prod(dims)
            v = low[:, at:at + n]
            if len(dims) == 2:
                v = v.rearrange("p (a b) -> p a b", a=dims[0])
            elif len(dims) == 3:
                v = v.rearrange("p (a b c) -> p a b c", a=dims[0], b=dims[1])
            return v

        xrow = view(0, NT, D)
        z = view(4096, NT, D)
        wnat = view(4096, CD, D)
        ring = view(8192, 4, L)
        normed = view(8192, TB, D)
        pre = view(9216, TB, D)
        gT = view(10240, CD, BLK)
        preT = view(11264, CD, BLK)
        stage = view(12288, CI, BLK + 4)
        xdbl = view(14400, BLK)
        win_sb = view(16384, CD, 2 * DI)
        wT = view(18432, CD, D)
        gb_bc = view(18944, D)
        wx_sb = view(19200, CI, XD)
        wdt_sb = view(19456, DI)
        wout_sb = view(21504, CI, D)
        ones = view(22528, BLK)
        rsum = view(0, CI, BLK)
        bu = view(2048, 2, 2, BLK)
        bc = view(4096, 2, 2, BLK)
        gate = view(6144, 2, 2, BLK)
        gate_all = view(6144, CI, BLK)
        yc = view(8192, 2, 2, BLK)
        hT = view(10240, 2, CI, BLK)
        yg = view(10240, CI, BLK)
        gateT = view(12288, BLK)
        xmT = view(14336, CD, BLK)
        w1_sb = view(15360, 2, CD * DI)
        w2_sb = view(17408, 2, CI * D)
        acc = view(19456, TB, D)
        xm = view(20480, TB, D)

        ident = sb("ident", [P, P])
        rowsum = sb("rowsum", [P, NT])
        deg = sb("deg", [P, NT])
        stats = sb("stats", [P, NT, 6])
        mv = sb("mv", [P, NT, 2])
        sa, sb_, sc_, sd_ = (sb(f"small{i}", [P, NT]) for i in range(4))
        zscale = sb("zscale", [P, NT])
        zbias = sb("zbias", [P, NT])
        stats2 = sb("stats2", [P, TB, 6])
        mv2 = sb("mv2", [P, TB, 2])
        q = sb("q", [P, 2 * TB])
        qr = sb("qr", [P, 2 * TB])
        qt = sb("qt", [P, 2 * TB])
        VECS = 2 * CD + 3 * CI + NE * CI
        vec_rows = sb("vec_rows", [VECS, P])
        vecs = sb("vecs", [P, VECS])
        w1c, w2c = vecs[:, 0:CD], vecs[:, CD:2 * CD]
        cb, bdt, dp = (vecs[:, 2 * CD + i * CI:2 * CD + (i + 1) * CI] for i in range(3))
        B1 = 2 * CD + 3 * CI
        cw = sb("cw", [P, CI, 4])
        amat = sb("amat", [P, CI, NS])
        ahalf = sb("ahalf", [P, CI, NS])
        carry = sb("carry", [P, CI, NS])
        tot = sb("tot", [P, CI, NB])
        suffix = sb("suffix", [P, CI, NB])
        eps_c = sb("eps_c", [P, 1])
        wg_sb = sb("wg_sb", [P, CD, NE])
        b2_sb = sb("b2_sb", [NE, D])
        ss = sb("ss", [P, TB])
        ssv = sb("ssv", [P, TB])
        r2 = sb("r2", [P, TB])
        r2t = sb("r2t", [P, TB])
        gw = sb("gw", [P, TB, 1 + NE])
        gmax = sb("gmax", [P, TB])
        gsum = sb("gsum", [P, TB])

        ps = ctx.enter_context(nc.psum_tensor("ps", [P, 8, BLK], F32))

        consts_loaded = sem("consts_loaded")
        x_loaded = sem("x_loaded")
        adj_loaded = [sem(f"adj_loaded{i}") for i in range(4)]
        pool_made = sem("pool_made")
        w_turned = sem("w_turned")
        w_kept = sem("w_kept")
        diag_added = sem("diag_added")
        row_summed = sem("row_summed")
        adj_turned = sem("adj_turned")
        adj_kept = sem("adj_kept")
        dve_a = sem("dve_a")
        act_a = sem("act_a")
        roots_a = sem("roots_a")
        z_made = sem("z_made")
        gcn_done = sem("gcn_done")
        gT_kept = sem("gT_kept")
        wmm_done = sem("wmm_done")
        q_made = sem("q_made")
        q_rooted = sem("q_rooted")
        dve_b = sem("dve_b")
        x1_made = sem("x1_made")
        pre_made = sem("pre_made")
        pre_turned = sem("pre_turned")
        preT_kept = sem("preT_kept")
        inproj_done = sem("inproj_done")
        inproj_used = sem("inproj_used")
        conv_done = sem("conv_done")
        u_made = sem("u_made")
        xdbl_done = sem("xdbl_done")
        xdbl_kept = sem("xdbl_kept")
        dt_done = sem("dt_done")
        act_soft = sem("act_soft")
        soft_made = sem("soft_made")
        delta_made = sem("delta_made")
        dt_abs = sem("dt_abs")
        dt_relu = sem("dt_relu")
        rows_saved = sem("rows_saved")
        bc_saved = sem("bc_saved")
        phase_a = sem("phase_a")
        skip_made = sem("skip_made")
        r_made = sem("r_made")
        dve_r = sem("dve_r")
        dve_c = sem("dve_c")
        bc_loaded = [sem(f"bc_loaded{i}") for i in range(2)]
        bu_made = sem("bu_made")
        a_made = sem("a_made")
        gate_made = sem("gate_made")
        scanned = sem("scanned")
        carried = sem("carried")
        guarded = sem("guarded")
        weighted = sem("weighted")
        summed = sem("summed")
        w1_loaded = [sem(f"w1_loaded{i}") for i in range(2)]
        w2_loaded = [sem(f"w2_loaded{i}") for i in range(2)]
        normed_loaded = sem("normed_loaded")
        gnn_loaded = sem("gnn_loaded")
        yg_made = sem("yg_made")
        mamba_done = sem("mamba_done")
        dve_p = sem("dve_p")
        v_made = sem("v_made")
        ss_made = sem("ss_made")
        ss_rooted = sem("ss_rooted")
        xm_made = sem("xm_made")
        xm_turned = sem("xm_turned")
        xmT_kept = sem("xmT_kept")
        gate_done = sem("gate_done")
        logit_made = sem("logit_made")
        gexp_made = sem("gexp_made")
        gw_made = sem("gw_made")
        gw_turned = sem("gw_turned")
        gateT_kept = sem("gateT_kept")
        hid_done = sem("hid_done")
        hid_kept = sem("hid_kept")
        hid_read = sem("hid_read")
        silu_made = sem("silu_made")
        exp_done = sem("exp_done")
        acc_made = sem("acc_made")
        acc_done = sem("acc_done")
        out_saved = sem("out_saved")

        block = ctx.enter_context(nc.Block())

        NP_CHUNK = NS * 2
        HEAD = 4
        BODY = 6
        STEPS = (NS - HEAD) // BODY
        SLOTS = 4
        assert (HEAD + STEPS * BODY, STEPS * SLOTS, BODY * 2) == (NS, NE, SLOTS * 3)
        NX = 2 + NE
        CONSTS = 16

        def xrow_block(k):
            return low[:, bass.ds(k * (TB * D), TB * D)].rearrange("p (t d) -> p t d", t=TB)

        @block.sync
        def _(sync):
            def const(to, of):
                sync.dma_start(to, of).then_inc(consts_loaded, 16)

            sync.dma_start(xrow, x.rearrange("(t p) d -> p t d", p=P)).then_inc(x_loaded, 16)

            def load_adj(t, s, first):
                if not first:
                    await_ge(sync, row_summed, t - 3)
                    await_ge(sync, adj_turned, 4 * (t - 3))
                sync.dma_start(ring[:, s, :], adj_t[t, :, :]).then_inc(adj_loaded[s], 16)

            for s in range(4):
                load_adj(s, s, True)
            const(wnat, gnn_w.rearrange("(a p) c -> p a c", p=P))
            const(win_sb, w_in.rearrange("(a p) n -> p a n", p=P))
            const(wx_sb, w_x.rearrange("(a p) n -> p a n", p=P))
            const(wdt_sb[0:DTR, :], w_dt)
            const(wout_sb, w_out.rearrange("(a p) n -> p a n", p=P))
            const(gb_bc, gnn_b.partition_broadcast(P))
            at = 0
            for v in (w_rms1, w_rms2, conv_b, b_dt, d_skip, b1.rearrange("e n -> (e n)")):
                rows = v.shape[0] // P
                const(vec_rows[at:at + rows, :], v.rearrange("(a p) -> a p", p=P))
                at += rows
            const(cw[:, :, :], conv_w.rearrange("(a p) o k -> p a (o k)", p=P))
            const(amat[:, :, :], a_log.rearrange("(a p) n -> p a n", p=P))
            const(wg_sb[:, :, :], w_gate.rearrange("(a p) n -> p a n", p=P))
            const(b2_sb[:, :], b2)
            with sync.Fori(1, NT // 4) as it:
                for s in range(4):
                    load_adj(4 * it + s, s, False)

            def save(k):
                await_ge(sync, x1_made, k + 1)
                sync.dma_start(gnn_rows.rearrange("(k t p) d -> k p t d", p=P, t=TB)[k],
                               xrow_block(k)).then_inc(rows_saved, 16)
                await_ge(sync, pre_made, TB * (k + 1))
                sync.dma_start(norm_rows.rearrange("(k t p) d -> k p t d", p=P, t=TB)[k],
                               normed).then_inc(rows_saved, 16)
                await_ge(sync, xdbl_kept, k + 1)
                sync.dma_start(bc_rows.rearrange("n (k l) -> k n l", k=NB)[k],
                               xdbl[DTR:XD, :]).then_inc(bc_saved, 16)

            with sync.Fori(0, NB) as k:
                save(k)

            await_ge(sync, bc_saved, 16 * NB)
            await_ge(sync, rows_saved, 32 * NB)
            sync.wait_ge(phase_a, 4)

            def load_bc(c, n, s, first):
                if not first:
                    await_ge(sync, bu_made, NP_CHUNK * c + 2 * (n - 1))
                    await_ge(sync, weighted, NP_CHUNK * c + 2 * (n - 1))
                sync.dma_start(bc[:, s, :, :],
                               bc_rows.rearrange("(a n) (k l) -> k n a l", a=2, k=NB)[c, n]
                               .partition_broadcast(P)).then_inc(bc_loaded[s], 16)

            def load_rows(c, first):
                if not first:
                    await_ge(sync, out_saved, 16 * c)
                sync.dma_start(acc, norm_rows.rearrange("(k t p) d -> k p t d", p=P, t=TB)[c])\
                    .then_inc(normed_loaded, 16)

            def load_gnn(c):
                await_ge(sync, xm_turned, c + 1)
                sync.dma_start(xm, gnn_rows.rearrange("(k t p) d -> k p t d", p=P, t=TB)[c])\
                    .then_inc(gnn_loaded, 16)

            def store(c):
                await_ge(sync, acc_done, c + 1)
                sync.dma_start(out.rearrange("(k t p) d -> k p t d", p=P, t=TB)[c], acc)\
                    .then_inc(out_saved, 16)

            def head(c, first):
                for n in range(2):
                    load_bc(c, n, n, first)
                if not first:
                    store(c - 2)
                    load_rows(c - 1, False)
                for n in range(2, HEAD):
                    load_bc(c, n, n % 2, False)

            def rest(c):
                with sync.Fori(0, STEPS) as g:
                    for i in range(BODY):
                        load_bc(c, HEAD + BODY * g + i, i % 2, False)

            head(0, True)
            load_rows(0, True)
            rest(0)
            for n in range(HEAD):
                load_bc(1, n, n % 2, False)
            load_gnn(0)
            rest(1)
            with sync.Fori(2, NB) as c:
                head(c, False)
                load_gnn(c - 1)
                rest(c)
            store(NB - 2)
            load_rows(NB - 1, False)
            load_gnn(NB - 1)
            store(NB - 1)
            await_ge(sync, out_saved, 16 * NB)

        @block.gpsimd
        def _(pool):
            pool.memset(ident[:, :], 0.0).then_inc(pool_made, 1)
            pool.wait_ge(pool_made, 1)
            pool.affine_select(out=ident[:, :], in_=ident[:, :], compare_op=ALU.not_equal, fill=1.0,
                               base=0, pattern=[[-1, P]], channel_multiplier=1).then_inc(pool_made, 1)
            pool.memset(ones, 1.0).then_inc(pool_made, 1)
            pool.memset(eps_c[:, :], EPS).then_inc(pool_made, 1)
            pool.memset(carry[:, :, :], 0.0).then_inc(pool_made, 1)
            pool.memset(gw[:, :, 0:1], 1.0).then_inc(pool_made, 1)
            pool.wait_ge(pool_made, 6)
            pool.nop().then_inc(phase_a, 1)

            def b_times(c, n, s, hf, first):
                pair = NP_CHUNK * c + 2 * n + hf
                if hf == 0:
                    await_ge(pool, bc_loaded[s], 16 * (c * (NS // 2) + (n - s) // 2 + 1))
                if not first:
                    await_ge(pool, scanned, 2 * (pair - 1))
                pool.tensor_tensor(bu[:, hf, :, :],
                                   arena[:, c, S0 + 2 * hf:S0 + 2 * hf + 2, :],
                                   bc[:, s, 0:1, :].broadcast_to([P, 2, BLK]), ALU.mult)\
                    .then_inc(bu_made, 1)

            def add_up(c, n, hf):
                pair = NP_CHUNK * c + 2 * n + hf
                await_ge(pool, weighted, pair + 1)
                y = arena[:, c, U0 + 2 * hf:U0 + 2 * hf + 2, :]
                pool.tensor_tensor(y, y, yc[:, hf, :, :], ALU.add).then_inc(summed, 1)

            pool.wait_ge(phase_a, 4)
            await_ge(pool, delta_made, CI * NB)
            await_ge(pool, skip_made, NB)

            def chunk(c, first):
                for n in range(4):
                    for hf in range(2):
                        b_times(c, n, n % 2, hf, first and n == 0)
                        if n:
                            add_up(c, n - 1, hf)
                        elif not first:
                            add_up(c - 1, NS - 1, hf)
                with pool.Fori(1, NS // 4) as g:
                    for n in range(4):
                        for hf in range(2):
                            b_times(c, 4 * g + n, n % 2, hf, False)
                            add_up(c, 4 * g + n - 1, hf)

            chunk(0, True)
            with pool.Fori(1, NB) as c:
                chunk(c, False)
            for hf in range(2):
                add_up(NB - 1, NS - 1, hf)

        @block.tensor
        def _(pe):
            pe.wait_ge(pool_made, 2)
            pe.wait_ge(consts_loaded, 16 * CONSTS)
            for a in range(CD):
                for c in range(CD):
                    ins = pe.transpose(ps[:, 0, (c * CD + a) * P:(c * CD + a + 1) * P],
                                       wnat[:, a, c * P:(c + 1) * P], ident[:, :])
            ins = pe.transpose(ps[:, 1, 0:VECS], vec_rows[:, :], ident[0:VECS, 0:VECS])
            ins.then_inc(w_turned, 1)
            pe.wait_ge(w_kept, 2)

            def turn_rows(t, s, first):
                pe.wait_ge(diag_added, t + 1)
                for b in range(4):
                    if not first:
                        pe.wait_ge(adj_kept, 4 * (t - 2) + b + 1)
                    for j in range(4):
                        ins = pe.transpose(ps[:, 4 * (s % 2) + b, j * P:(j + 1) * P],
                                           ring[:, s, (4 * b + j) * P:(4 * b + j + 1) * P], ident[:, :])
                    ins.then_inc(adj_turned, 1)

            for s in range(4):
                turn_rows(s, s, s < 2)
            with pe.Fori(1, NT // 4) as it:
                for s in range(4):
                    turn_rows(4 * it + s, s, False)

            S_, W_, T_, I_ = 0, 2, 4, 6

            def gcn(k, c):
                for j in range(NT):
                    ins = pe.matmul(ps[:, S_ + c, :], z[:, j, c * P:(c + 1) * P], arena[:, k, j, :],
                                    start=(j == 0), stop=(j == NT - 1))
                ins.then_inc(gcn_done, 1)

            pe.wait_ge(adj_kept, 4 * NT)
            pe.wait_ge(z_made, NT)
            gcn(0, 0)
            gcn(0, 1)

            def block_a(k, first, last):
                pe.wait_ge(gT_kept, 2 * (k + 1))
                for t in range(TB):
                    for c in range(CD):
                        ins = pe.matmul(ps[:, W_ + t // 2, (t % 2) * D:(t % 2 + 1) * D],
                                        gT[:, c, t * P:(t + 1) * P], wT[:, c, :],
                                        start=(c == 0 and t % 2 == 0), stop=(c == CD - 1),
                                        skip_group_check=True)
                    ins.then_inc(wmm_done, 1)
                if not last:
                    gcn(k + 1, 0)
                for t in range(TB):
                    pe.wait_ge(pre_made, TB * k + t + 1)
                    if t == 0 and not first:
                        pe.wait_ge(dt_relu, CI * k)
                    for c in range(CD):
                        ins = pe.transpose(ps[:, T_ + c, t * P:(t + 1) * P],
                                           pre[:, t, c * P:(c + 1) * P], ident[:, :])
                ins.then_inc(pre_turned, 1)
                pe.wait_ge(preT_kept, 2 * (k + 1))
                for m in range(2 * CI):
                    if m >= 2:
                        pe.wait_ge(inproj_used, 2 * CI * k + m - 1)
                    elif not first:
                        pe.wait_ge(dt_relu, CI * k)
                    for c in range(CD):
                        ins = pe.matmul(ps[:, I_ + m % 2, :], win_sb[:, c, m * P:(m + 1) * P],
                                        preT[:, c, :], start=(c == 0), stop=(c == CD - 1))
                    ins.then_inc(inproj_done, 1)
                if not last:
                    gcn(k + 1, 1)
                for c in range(CI):
                    pe.wait_ge(u_made, CI * k + c + 1)
                    ins = pe.matmul(ps[0:XD, W_, :], wx_sb[:, c, :], arena[:, k, U0 + c, :],
                                    start=(c == 0), stop=(c == CI - 1))
                ins.then_inc(xdbl_done, 1)
                pe.wait_ge(xdbl_kept, k + 1)
                for m in range(CI):
                    pe.matmul(ps[:, T_ + m, :], wdt_sb[0:DTR, m * P:(m + 1) * P], xdbl[0:DTR, :],
                              start=True, stop=True).then_inc(dt_done, 1)

            block_a(0, True, False)
            with pe.Fori(1, NB - 1) as k:
                block_a(k, False, False)
            block_a(NB - 1, False, True)
            pe.wait_ge(dt_done, CI * NB)
            pe.nop().then_inc(phase_a, 1)
            pe.wait_ge(phase_a, 4)

            O_, M_ = 4, 6

            def prep(c, first):
                pe.wait_ge(yg_made, c + 1)
                for t in range(TB):
                    if t % 2 == 0 and not first:
                        pe.wait_ge(acc_made, TB * (NX * c - 1) + t + 2)
                    for m in range(CI):
                        ins = pe.matmul(ps[:, O_ + t // 2, (t % 2) * D:(t % 2 + 1) * D],
                                        yg[:, m, t * P:(t + 1) * P], wout_sb[:, m, :],
                                        start=(m == 0 and t % 2 == 0), stop=(m == CI - 1),
                                        skip_group_check=True)
                ins.then_inc(mamba_done, 1)
                for t in range(TB):
                    pe.wait_ge(xm_made, TB * c + t + 1)
                    if t == 0 and not first:
                        pe.wait_ge(silu_made, 3 * NE * c)
                    for a in range(CD):
                        ins = pe.transpose(ps[:, M_ + a, t * P:(t + 1) * P],
                                           xm[:, t, a * P:(a + 1) * P], ident[:, :])
                ins.then_inc(xm_turned, 1)
                pe.wait_ge(xmT_kept, 2 * (c + 1))
                for t in range(TB):
                    for a in range(CD):
                        ins = pe.matmul(ps[:, O_, t * NE:(t + 1) * NE], xmT[:, a, t * P:(t + 1) * P],
                                        wg_sb[:, a, :], start=(a == 0 and t == 0), stop=(a == CD - 1),
                                        skip_group_check=True)
                ins.then_inc(gate_done, 1)
                pe.wait_ge(gw_made, c + 1)
                for t in range(TB):
                    ins = pe.transpose(ps[0:NE, O_ + 1, t * P:(t + 1) * P], gw[:, t, 1:], ident[:, :])
                ins.then_inc(gw_turned, 1)
                pe.wait_ge(gateT_kept, c + 1)
                for t in range(TB):
                    pe.matmul(ps[:, O_ + t // 2, (t % 2) * D:(t % 2 + 1) * D],
                              gateT[0:NE, t * P:(t + 1) * P], b2_sb[:, :],
                              start=(t % 2 == 0), stop=True, skip_group_check=True)\
                        .then_inc(exp_done, 1)

            def first_layer(c, e, s, half):
                count = NE * c + e
                if half == 0:
                    pe.wait_ge(w1_loaded[s], 16 * (c * (NE // 2) + (e - s) // 2 + 1))
                for m in range(2 * half, 2 * half + 2):
                    if half:
                        pe.wait_ge(hid_read, 2 * count + m - 1)
                    elif isinstance(e, int) and e == 0:
                        pe.wait_ge(xmT_kept, 2 * (c + 1))
                    else:
                        pe.wait_ge(silu_made, 3 * (count - 1) + m + 1)
                    for a in range(CD):
                        ins = pe.matmul(ps[:, M_ + m % 2, :],
                                        w1_sb[:, s, a * DI + m * P:a * DI + (m + 1) * P],
                                        xmT[:, a, :], start=(a == 0), stop=(a == CD - 1))
                    ins.then_inc(hid_done, 1)

            def second_layer(c, e, s, half):
                if half == 0:
                    pe.wait_ge(silu_made, 3 * (NE * c + e + 1))
                    pe.wait_ge(w2_loaded[s], 16 * (c * (NE // 2) + (e - s) // 2 + 1))
                pe.wait_ge(acc_made, TB * (NX * c + 1 + e) + 2 * half + 2)
                for t in range(2 * half, 2 * half + 2):
                    for m in range(CI):
                        ins = pe.matmul(ps[:, O_ + half, (t % 2) * D:(t % 2 + 1) * D],
                                        hT[:, s, m, t * P:(t + 1) * P], w2_sb[:, s, m * D:(m + 1) * D],
                                        start=(m == 0 and t % 2 == 0), stop=(m == CI - 1),
                                        skip_group_check=True)
                    ins.then_inc(exp_done, 1)

            def layers(c, e, s):
                first_layer(c, e, s, 0)
                second_layer(c, e - 1, 1 - s, 0)
                first_layer(c, e, s, 1)
                second_layer(c, e - 1, 1 - s, 1)

            def experts(c):
                for half in range(2):
                    first_layer(c, 0, 0, half)
                layers(c, 1, 1)
                with pe.Fori(1, NE // 2) as g:
                    for s in range(2):
                        layers(c, 2 * g + s, s)
                for half in range(2):
                    second_layer(c, NE - 1, 1, half)

            prep(0, True)
            experts(0)
            with pe.Fori(1, NB) as c:
                prep(c, False)
                experts(c)

        @block.scalar
        def _(act):
            act.wait_ge(w_turned, 1)
            act.activation(wT, ps[:, 0, :].rearrange("p (a n) -> p a n", a=CD), ACT.Copy)\
                .then_inc(w_kept, 1)
            act.activation(vecs[:, :], ps[:, 1, 0:VECS], ACT.Copy).then_inc(w_kept, 1)

            def keep_rows(t, s):
                blk = (t - s) // 4 if isinstance(t, int) else t_block
                for b in range(4):
                    await_ge(act, adj_turned, 4 * t + b + 1)
                    act.activation(arena[:, blk, 4 * b:4 * b + 4, s * P:(s + 1) * P],
                                   ps[:, 4 * (s % 2) + b, :].rearrange("p (j i) -> p j i", j=4),
                                   ACT.Copy).then_inc(adj_kept, 1)

            t_block = 0
            for s in range(4):
                keep_rows(s, s)
            with act.Fori(1, NT // 4) as it:
                t_block = it
                for s in range(4):
                    keep_rows(4 * it + s, s)

            await_ge(act, row_summed, NT)
            act.wait_ge(pool_made, 6)
            act.activation(sa[:, :], rowsum[:, :], ACT.Sqrt).then_inc(roots_a, 1)
            act.wait_ge(dve_a, 1)
            act.activation(sb_[:, :], mv[:, :, 1], ACT.Sqrt, bias=eps_c[:, :]).then_inc(roots_a, 1)
            await_ge(act, consts_loaded, 16 * CONSTS)
            act.activation(amat[:, :, :], amat[:, :, :], ACT.Exp).then_inc(act_a, 1)
            act.wait_ge(act_a, 1)
            act.activation(ahalf[:, :, :], amat[:, :, :], ACT.Copy, scale=-0.5).then_inc(act_a, 1)
            act.wait_ge(act_a, 2)
            act.activation(amat[:, :, :], amat[:, :, :], ACT.Copy, scale=-1.0).then_inc(act_a, 1)

            S_, W_, T_, I_ = 0, 2, 4, 6

            def block_a(k, first):
                await_ge(act, gcn_done, 2 * k + 1)
                if not first:
                    await_ge(act, wmm_done, TB * k)
                act.activation(gT[:, 0, :], ps[:, S_, :], ACT.Copy).then_inc(gT_kept, 1)
                await_ge(act, q_made, k + 1)
                act.activation(qr[:, :], q[:, :], ACT.Sqrt).then_inc(q_rooted, 1)
                await_ge(act, pre_turned, k + 1)
                act.activation(preT[:, 0, :], ps[:, T_, :], ACT.Copy, scale=w1c[:, 0:1])\
                    .then_inc(preT_kept, 1)
                for m in range(CI):
                    await_ge(act, inproj_done, 2 * CI * k + m + 1)
                    if m == 0 and not first:
                        await_ge(act, conv_done, (CI + 1) * k + 1)
                    act.activation(stage[:, m, 3:3 + BLK], ps[:, I_ + m % 2, :], ACT.Copy)\
                        .then_inc(inproj_used, 1)
                for m in range(CI):
                    await_ge(act, inproj_done, 2 * CI * k + CI + m + 1)
                    act.activation(arena[:, k, G0 + m, :], ps[:, I_ + m % 2, :], ACT.Silu)\
                        .then_inc(inproj_used, 1)
                for m in range(CI):
                    await_ge(act, conv_done, (CI + 1) * k + m + 2)
                    act.activation(arena[:, k, U0 + m, :], arena[:, k, U0 + m, :], ACT.Silu,
                                   bias=cb[:, m:m + 1]).then_inc(u_made, 1)
                await_ge(act, xdbl_done, k + 1)
                if not first:
                    await_ge(act, bc_saved, 16 * k)
                act.activation(xdbl[0:XD, :], ps[0:XD, W_, :], ACT.Copy).then_inc(xdbl_kept, 1)
                for m in range(CI):
                    await_ge(act, dt_done, CI * k + m + 1)
                    act.activation(arena[:, k, D0 + m, :], ps[:, T_ + m, :], ACT.Abs,
                                   bias=bdt[:, m:m + 1]).then_inc(dt_abs, 1)
                dl = arena[:, k, D0:D0 + CI, :]
                await_ge(act, dt_abs, CI * (k + 1))
                act.activation(dl, dl, ACT.Exp, scale=-1.0).then_inc(act_soft, 1)
                await_ge(act, act_soft, k + 1)
                act.activation(dl, dl, ACT.Ln, bias=1.0).then_inc(soft_made, 1)

            block_a(0, True)
            with act.Fori(1, NB) as k:
                block_a(k, False)
            await_ge(act, soft_made, NB)
            act.activation(gmax[:, 0:1], eps_c[:, :], ACT.Exp).then_inc(phase_a, 1)
            act.wait_ge(phase_a, 4)
            act.wait_ge(act_a, 3)

            def load_w1(e, s):
                act.dma_start(w1_sb[:, s, :].rearrange("p (a n) -> p a n", a=CD),
                              w1.rearrange("e (a p) n -> e p a n", p=P)[e]).then_inc(w1_loaded[s], 16)

            def load_w2(e, s):
                act.dma_start(w2_sb[:, s, :].rearrange("p (a n) -> p a n", a=CI),
                              w2.rearrange("e (a p) n -> e p a n", p=P)[e]).then_inc(w2_loaded[s], 16)

            def decay(c, n, hf, first, new_chunk=False):
                pair = NP_CHUNK * c + 2 * n + hf
                if not first:
                    await_ge(act, weighted, pair - 1)
                for j in range(2):
                    m = 2 * hf + j
                    act.activation(ps[:, m, :], arena[:, c, D0 + m, :], ACT.Exp,
                                   scale=amat[:, m, bass.ds(n, 1)]).then_inc(a_made, 1)
                if new_chunk:
                    await_ge(act, r_made, c + 1)
                for j in range(2):
                    m = 2 * hf + j
                    act.activation(gate[:, hf, j, :], rsum[:, m, :], ACT.Tanh,
                                   scale=ahalf[:, m, bass.ds(n, 1)], bias=-0.5 * math.log(SCAN_EPS))\
                        .then_inc(gate_made, 1)

            def hidden(c, e, s):
                count = NE * c + e
                for m in range(2, CI):
                    await_ge(act, hid_done, CI * count + m + 1)
                    act.activation(hT[:, s, m, :], ps[:, 6 + m % 2, :], ACT.Silu,
                                   bias=vecs[:, bass.ds(B1 + CI * e + m, 1)]).then_inc(silu_made, 1)
                await_ge(act, hid_read, 2 * count + 2)
                act.activation(hT[:, s, 0:2, :], hT[:, s, 0:2, :], ACT.Silu).then_inc(silu_made, 1)

            def squares(c):
                await_ge(act, v_made, c + 1)
                for t in range(TB):
                    act.activation(xm[:, t, :], acc[:, t, :], ACT.Square, accum_out=ss[:, t:t + 1])\
                        .then_inc(ss_made, 1)
                await_ge(act, ss_made, TB * (c + 1))
                act.activation(r2[:, :], ss[:, :], ACT.Sqrt, scale=1.0 / D, bias=eps_c[:, :])\
                    .then_inc(ss_rooted, 1)

            def keep_xmT(c):
                await_ge(act, xm_turned, c + 1)
                act.activation(xmT[:, 0, :], ps[:, 6, :], ACT.Copy, scale=w2c[:, 0:1])\
                    .then_inc(xmT_kept, 1)

            def gate_exp(c):
                await_ge(act, logit_made, c + 1)
                act.activation(gw[:, :, 1:], gw[:, :, 1:], ACT.Exp).then_inc(gexp_made, 1)

            def chunk(c, first_chunk):
                for q in range(2 * HEAD):
                    decay(c, q // 2, q % 2, first_chunk and q < 2, q == 0)
                    if not first_chunk:
                        if q == 4:
                            squares(c - 1)
                        elif q == 6:
                            keep_xmT(c - 1)
                        elif q == 7:
                            gate_exp(c - 1)
                with act.Fori(0, STEPS) as g:
                    for q in range(2 * BODY):
                        decay(c, HEAD + BODY * g + q // 2, q % 2, False)
                        if first_chunk:
                            continue
                        i = q // 3
                        e = SLOTS * g + i
                        if q % 3 == 0:
                            await_ge(act, hid_done, CI * (NE * (c - 1) + e) + 1)
                            load_w2(e, i % 2)
                        elif q % 3 == 2:
                            hidden(c - 1, e, i % 2)
                            load_w1(e + 2 if i < 2 else SLOTS * (STEPS - 1 - g) + i - 2, i % 2)

            chunk(0, True)
            for s in range(2):
                load_w1(s, s)
            with act.Fori(1, NB) as c:
                chunk(c, False)
            c = NB - 1
            squares(c)
            keep_xmT(c)
            gate_exp(c)

            def expert(e, s, more):
                await_ge(act, hid_done, CI * (NE * c + e) + 1)
                load_w2(e, s)
                hidden(c, e, s)
                if more:
                    load_w1(e + 2, s)

            with act.Fori(0, NE // 2 - 1) as g:
                for s in range(2):
                    expert(2 * g + s, s, True)
            for s in range(2):
                expert(NE - 2 + s, s, False)

        @block.vector
        def _(dve):
            dve.wait_ge(x_loaded, 16)
            for t in range(NT):
                dve.bn_stats(stats[:, t, :], xrow[:, t, :]).then_inc(dve_r, 1)
            await_ge(dve, dve_r, NT)
            for t in range(NT):
                ins = dve.bn_aggr(mv[:, t, :], stats[:, t, :])
            ins.then_inc(dve_a, 1)
            dve.wait_ge(pool_made, 2)

            def sum_rows(t, s, loaded):
                await_ge(dve, adj_loaded[s], 16 * loaded)
                d = ring[:, s, bass.ds(t * P, P)]
                dve.tensor_tensor(d, d, ident[:, :], ALU.add).then_inc(diag_added, 1)
                await_ge(dve, diag_added, t + 1)
                dve.tensor_reduce(rowsum[:, bass.ds(t, 1)], ring[:, s, :], AX, ALU.add)\
                    .then_inc(row_summed, 1)

            for s in range(4):
                sum_rows(s, s, 1)
            with dve.Fori(1, NT // 4) as it:
                for s in range(4):
                    sum_rows(4 * it + s, s, it + 1)

            a = Steps(dve, dve_a, 0)
            a.n = 1

            def newton(st, y, v, tmp):
                st.did(dve.tensor_tensor(tmp, y, y, ALU.mult))
                st.wait()
                st.did(dve.tensor_tensor(tmp, tmp, v, ALU.mult))
                st.wait()
                st.did(dve.tensor_scalar(tmp, tmp, -0.5, 1.5, ALU.mult, ALU.add))
                st.wait()
                st.did(dve.tensor_tensor(y, y, tmp, ALU.mult))
                st.wait()

            dve.wait_ge(roots_a, 2)
            await_ge(dve, row_summed, NT)
            a.did(dve.reciprocal(deg[:, :], sa[:, :]))
            a.did(dve.reciprocal(zscale[:, :], sb_[:, :]))
            a.did(dve.tensor_scalar(sd_[:, :], mv[:, :, 1], EPS, None, ALU.add))
            a.wait()
            newton(a, deg[:, :], rowsum[:, :], sc_[:, :])
            newton(a, zscale[:, :], sd_[:, :], sc_[:, :])
            a.did(dve.tensor_tensor(zscale[:, :], zscale[:, :], deg[:, :], ALU.mult))
            a.wait()
            for t in range(NT):
                dve.tensor_scalar(z[:, t, :], xrow[:, t, :], mv[:, t, 0:1], zscale[:, t:t + 1],
                                  ALU.subtract, ALU.mult).then_inc(z_made, 1)
            dve.memset(stage[:, :, 0:3], 0.0).then_inc(conv_done, 1)

            S_, W_, T_, I_ = 0, 2, 4, 6

            def block_a(k, first):
                st = Steps(dve, dve_b, k * STEPS_A)
                await_ge(dve, gcn_done, 2 * k + 2)
                if not first:
                    await_ge(dve, wmm_done, TB * k)
                dve.tensor_copy(gT[:, 1, :], ps[:, S_ + 1, :]).then_inc(gT_kept, 1)
                if not first:
                    await_ge(dve, rows_saved, 32 * k)
                xb = xrow_block(k)
                for t in range(TB):
                    await_ge(dve, wmm_done, TB * k + 2 * (t // 2) + 2)
                    st.did(dve.scalar_tensor_tensor(
                        normed[:, t, :], ps[:, W_ + t // 2, (t % 2) * D:(t % 2 + 1) * D],
                        deg[:, bass.ds(TB * k + t, 1)], gb_bc, ALU.mult, ALU.add))
                for t in range(TB):
                    st.wait(TB - 1)
                    st.did(dve.scalar_tensor_tensor(
                        xb[:, t, :], normed[:, t, :], 0.0, xb[:, t, :], ALU.max, ALU.add))
                for t in range(TB):
                    st.wait(TB - 1)
                    st.did(dve.bn_stats(stats2[:, t, :], xb[:, t, :]))
                for t in range(TB):
                    st.wait(TB - 1)
                    st.did(dve.bn_aggr(mv2[:, t, :], stats2[:, t, :]))
                st.wait()
                st.did(dve.tensor_scalar(q[:, 0:TB], mv2[:, :, 1], EPS, None, ALU.add))
                st.wait()
                dve.scalar_tensor_tensor(q[:, TB:], q[:, 0:TB], EPS, mv2[:, :, 1], ALU.mult, ALU.add)\
                    .then_inc(q_made, 1)
                await_ge(dve, q_made, k + 1)
                dve.nop().then_inc(x1_made, 1)
                await_ge(dve, q_rooted, k + 1)
                st.did(dve.reciprocal(qr[:, :], qr[:, :]))
                st.wait()
                newton(st, qr[:, :], q[:, :], qt[:, :])
                for t in range(TB):
                    dve.tensor_scalar(pre[:, t, :], xb[:, t, :], mv2[:, t, 0:1],
                                      qr[:, TB + t:TB + t + 1], ALU.subtract, ALU.mult)
                    dve.tensor_scalar(normed[:, t, :], xb[:, t, :], mv2[:, t, 0:1], qr[:, t:t + 1],
                                      ALU.subtract, ALU.mult).then_inc(pre_made, 1)
                await_ge(dve, pre_turned, k + 1)
                dve.tensor_scalar(preT[:, 1, :], ps[:, T_ + 1, :], w1c[:, 1:2], None, ALU.mult)\
                    .then_inc(preT_kept, 1)
                for m in range(CI):
                    await_ge(dve, inproj_used, 2 * CI * k + m + 1)
                    o = arena[:, k, U0 + m, :]
                    st.did(dve.tensor_scalar(o, stage[:, m, 0:BLK], cw[:, m, 0:1], None, ALU.mult))
                    for j in range(1, 4):
                        st.wait()
                        ins = dve.scalar_tensor_tensor(o, stage[:, m, j:j + BLK], cw[:, m, j:j + 1],
                                                       o, ALU.mult, ALU.add)
                        if j < 3:
                            st.did(ins)
                        else:
                            ins.then_inc(conv_done, 1)
                await_ge(dve, conv_done, (CI + 1) * k + CI + 1)
                dve.tensor_copy(stage[:, :, 0:3], stage[:, :, BLK:BLK + 3]).then_inc(conv_done, 1)
                for m in range(CI):
                    await_ge(dve, dt_done, CI * k + m + 1)
                    await_ge(dve, dt_abs, CI * k + m + 1)
                    dve.tensor_scalar(arena[:, k, S0 + m, :], ps[:, T_ + m, :], bdt[:, m:m + 1], 0.0,
                                      ALU.add, ALU.max).then_inc(dt_relu, 1)
                await_ge(dve, soft_made, k + 1)
                await_ge(dve, dt_relu, CI * (k + 1))
                for m in range(CI):
                    d = arena[:, k, D0 + m, :]
                    st.did(dve.scalar_tensor_tensor(d, arena[:, k, S0 + m, :], 1.0, d, ALU.mult,
                                                    ALU.add, accum_out=tot[:, m, bass.ds(k, 1)]))
                for m in range(CI):
                    st.wait(CI - 1)
                    st.did(dve.scalar_tensor_tensor(arena[:, k, S0 + m, :], arena[:, k, D0 + m, :],
                                                    0.5, arena[:, k, U0 + m, :], ALU.mult, ALU.mult))
                await_ge(dve, xdbl_done, k + 1)
                for m in range(CI):
                    st.wait(CI - 1)
                    u = arena[:, k, U0 + m, :]
                    st.did(dve.tensor_scalar(u, u, dp[:, m:m + 1], None, ALU.mult))
                st.wait()
                dve.nop().then_inc(skip_made, 1)
                return st.n

            STEPS_A = 4 * TB + 1 + 1 + 4 + 3 * CI + 3 * CI
            assert block_a(0, True) == STEPS_A
            with dve.Fori(1, NB) as k:
                block_a(k, False)
            st = Steps(dve, dve_b, NB * STEPS_A)
            st.did(dve.memset(suffix[:, :, NB - 1], 0.0))
            for k in range(NB - 2, -1, -1):
                st.wait()
                st.did(dve.tensor_tensor(suffix[:, :, k], suffix[:, :, k + 1], tot[:, :, k + 1],
                                         ALU.add))
            st.wait()
            dve.nop().then_inc(delta_made, CI * NB)
            dve.nop().then_inc(phase_a, 1)
            dve.wait_ge(phase_a, 4)

            def make_r(c):
                dve.tensor_copy(gate_all, arena[:, c, D0:D0 + CI, :]).then_inc(dve_c, 1)
                dve.tensor_copy(rsum[:, :, BLK - 1:BLK], suffix[:, :, bass.ds(c, 1)])
                await_ge(dve, dve_c, c + 1)
                for m in range(CI):
                    ins = dve.tensor_tensor_scan(
                        rsum[:, m, 0:BLK - 1][:, ::-1], ones[:, 0:BLK - 1],
                        gate_all[:, m, 1:BLK][:, ::-1], suffix[:, m, bass.ds(c, 1)],
                        ALU.mult, ALU.add)
                ins.then_inc(r_made, 1)

            def scans(c, n, hf, first_chunk):
                pair = NP_CHUNK * c + 2 * n + hf
                await_ge(dve, bu_made, pair + 1)
                if not first_chunk and hf == 0:
                    await_ge(dve, carried, NP_CHUNK * (c - 1) + 2 * n + 2)
                for j in range(2):
                    m = 2 * hf + j
                    await_ge(dve, a_made, 2 * pair + j + 1)
                    dve.tensor_tensor_scan(ps[:, m, :], ps[:, m, :], bu[:, hf, j, :],
                                           carry[:, m, bass.ds(n, 1)], ALU.mult, ALU.add)\
                        .then_inc(scanned, 1)

            def guard(c, n, hf):
                pair = NP_CHUNK * c + 2 * n + hf
                h = ps[:, 2 * hf:2 * hf + 2, :]
                await_ge(dve, scanned, 2 * pair + 2)
                dve.tensor_copy(carry[:, 2 * hf:2 * hf + 2, bass.ds(n, 1)],
                                ps[:, 2 * hf:2 * hf + 2, BLK - 1:BLK]).then_inc(carried, 1)
                await_ge(dve, gate_made, 2 * pair + 2)
                await_ge(dve, carried, pair + 1)
                dve.scalar_tensor_tensor(h, gate[:, hf, :, :], 1.0, h, ALU.add, ALU.mult)\
                    .then_inc(guarded, 1)

            def weigh(c, n, s, hf, first):
                pair = NP_CHUNK * c + 2 * n + hf
                await_ge(dve, guarded, pair + 1)
                if not first:
                    await_ge(dve, summed, pair - 1)
                dve.tensor_tensor(yc[:, hf, :, :], ps[:, 2 * hf:2 * hf + 2, :],
                                  bc[:, s, 1:2, :].broadcast_to([P, 2, BLK]), ALU.mult)\
                    .then_inc(weighted, 1)

            def pair(c, n, s, hf, first, first_chunk):
                if hf == 0:
                    await_ge(dve, bc_loaded[s], 16 * (c * (NS // 2) + (n - s) // 2 + 1))
                scans(c, n, hf, first_chunk)
                guard(c, n, hf)
                weigh(c, n, s, hf, first)

            def gate_y(c):
                await_ge(dve, summed, NP_CHUNK * (c + 1))
                dve.tensor_tensor(yg, arena[:, c, U0:U0 + CI, :], arena[:, c, G0:G0 + CI, :], ALU.mult)\
                    .then_inc(yg_made, 1)

            def add_norm(c):
                await_ge(dve, normed_loaded, 16 * (c + 1))
                await_ge(dve, mamba_done, c + 1)
                o = ps[:, 4:6, :].rearrange("p a (b d) -> p (a b) d", b=2)
                dve.tensor_tensor(acc, o, acc, ALU.add).then_inc(v_made, 1)

            def rms_norm(c):
                st = Steps(dve, dve_p, c * STEPS_P)
                await_ge(dve, ss_made, TB * (c + 1))
                st.did(dve.tensor_scalar(ssv[:, :], ss[:, :], 1.0 / D, EPS, ALU.mult, ALU.add))
                await_ge(dve, ss_rooted, c + 1)
                st.did(dve.reciprocal(r2[:, :], r2[:, :]))
                st.wait()
                newton(st, r2[:, :], ssv[:, :], r2t[:, :])
                await_ge(dve, v_made, c + 1)
                for t in range(TB):
                    dve.tensor_scalar(xm[:, t, :], acc[:, t, :], r2[:, t:t + 1], None, ALU.mult)\
                        .then_inc(xm_made, 1)
                return st.n

            def keep_xmT(c):
                await_ge(dve, xm_turned, c + 1)
                dve.tensor_scalar(xmT[:, 1, :], ps[:, 7, :], w2c[:, 1:2], None, ALU.mult)\
                    .then_inc(xmT_kept, 1)

            def gate_logits(c, at):
                st = Steps(dve, dve_p, c * STEPS_P)
                st.n = at
                await_ge(dve, gate_done, c + 1)
                lg = ps[:, 4, 0:TB * NE].rearrange("p (t e) -> p t e", t=TB)
                st.did(dve.tensor_reduce(gmax[:, :], lg, AX, ALU.max))
                st.wait()
                dve.tensor_tensor(gw[:, :, 1:], lg, gmax[:, :].unsqueeze(2).broadcast_to([P, TB, NE]),
                                  ALU.subtract).then_inc(logit_made, 1)
                return st.n

            def gate_weights(c, at):
                st = Steps(dve, dve_p, c * STEPS_P)
                st.n = at
                await_ge(dve, gexp_made, c + 1)
                st.did(dve.tensor_reduce(gsum[:, :], gw[:, :, 1:], AX, ALU.add))
                st.wait()
                st.did(dve.reciprocal(gsum[:, :], gsum[:, :]))
                st.wait()
                dve.tensor_tensor(gw[:, :, 1:], gw[:, :, 1:],
                                  gsum[:, :].unsqueeze(2).broadcast_to([P, TB, NE]), ALU.mult)\
                    .then_inc(gw_made, 1)
                await_ge(dve, gnn_loaded, 16 * (c + 1))
                dve.tensor_tensor(acc, acc, xm, ALU.add).then_inc(acc_made, TB)
                await_ge(dve, gw_turned, c + 1)
                dve.tensor_copy(gateT[0:NE, :], ps[0:NE, 5, :]).then_inc(gateT_kept, 1)
                return st.n

            def keep_hidden(c, e, s):
                count = NE * c + e
                for m in range(2):
                    await_ge(dve, hid_done, CI * count + m + 1)
                    dve.tensor_scalar(hT[:, s, m, :], ps[:, 6 + m, :],
                                      vecs[:, bass.ds(B1 + CI * e + m, 1)], None, ALU.add)\
                        .then_inc(hid_read, 1)

            def mix(c, x, half):
                count = (NE + 1) * c + x
                await_ge(dve, exp_done, TB * count + 2 * half + 2)
                await_ge(dve, acc_made, TB * (NX * c + x) + 2 * half + 2)
                for t in range(2 * half, 2 * half + 2):
                    dve.scalar_tensor_tensor(acc[:, t, :], ps[:, 4 + half, (t % 2) * D:(t % 2 + 1) * D],
                                             gw[:, t, bass.ds(x, 1)], acc[:, t, :],
                                             ALU.mult, ALU.add).then_inc(acc_made, 1)

            def last_mix(c):
                for half in range(2):
                    mix(c, NE, half)
                await_ge(dve, acc_made, TB * NX * (c + 1))
                dve.nop().then_inc(acc_done, 1)

            def chunk(c, first_chunk, last_open):
                at = 0
                make_r(c)
                for q in range(2 * HEAD):
                    n = q // 2
                    pair(c, n, n % 2, q % 2, first_chunk and n == 0, first_chunk)
                    if first_chunk:
                        continue
                    if q == 0:
                        if last_open:
                            last_mix(c - 2)
                        gate_y(c - 1)
                    elif q == 2:
                        add_norm(c - 1)
                    elif q == 4:
                        at = rms_norm(c - 1)
                    elif q == 5:
                        keep_xmT(c - 1)
                    elif q == 6:
                        at = gate_logits(c - 1, at)
                    elif q == 7:
                        assert gate_weights(c - 1, at) == STEPS_P
                with dve.Fori(0, STEPS) as g:
                    for q in range(2 * BODY):
                        n = HEAD + BODY * g + q // 2
                        pair(c, n, q // 2 % 2, q % 2, False, first_chunk)
                        if first_chunk:
                            continue
                        e = SLOTS * g + q // 3
                        if q % 3 == 0:
                            keep_hidden(c - 1, e, q // 3 % 2)
                        else:
                            mix(c - 1, e, q % 3 - 1)

            STEPS_P = 6 + 1 + 2
            chunk(0, True, False)
            chunk(1, False, False)
            with dve.Fori(2, NB) as c:
                chunk(c, False, True)
            c = NB - 1
            last_mix(c - 1)
            gate_y(c)
            add_norm(c)
            at = rms_norm(c)
            keep_xmT(c)
            at = gate_logits(c, at)
            gate_weights(c, at)

            def expert(e, s):
                keep_hidden(c, e, s)
                for half in range(2):
                    mix(c, e, half)

            expert(0, 0)
            expert(1, 1)
            with dve.Fori(1, NE // 2) as g:
                for s in range(2):
                    expert(2 * g + s, s)
            last_mix(c)


_INS = ['x', 'adj', 'L0_gnn_W', 'L0_gnn_b', 'L0_ffn_w_rms1', 'L0_ffn_w_rms2', 'L0_ffn_W_in',
        'L0_ffn_conv_w', 'L0_ffn_conv_b', 'L0_ffn_W_x', 'L0_ffn_W_dt', 'L0_ffn_b_dt', 'L0_ffn_A_log',
        'L0_ffn_Dp', 'L0_ffn_W_out', 'L0_ffn_W_gate', 'L0_ffn_W1', 'L0_ffn_b1', 'L0_ffn_W2',
        'L0_ffn_b2']


def kernel(**inputs):
    import numpy as np
    import concourse.bacc as bacc
    from concourse.bass_utils import run_bass_kernel_spmd

    nc = bacc.Bacc("TRN2", target_bir_lowering=False, num_devices=1, dynamic_dma_scratch_size=1024)
    arrays, args = {}, []
    for name in _INS:
        a = np.ascontiguousarray(inputs[name])
        arrays[f"in_{name}"] = a
        args.append(nc.dram_tensor(f"in_{name}", a.shape, mybir.dt.from_np(a.dtype),
                                   kind="ExternalInput").ap())
    out = nc.dram_tensor("out_rows", inputs['x'].shape, F32, kind="ExternalOutput").ap()
    build(nc, *args, out)
    r = run_bass_kernel_spmd(nc, [arrays], core_ids=[0])
    return r.results[0]["out_rows"]
```

```python
import math
from contextlib import ExitStack

import concourse.bass as bass
from concourse import mybir

F32 = mybir.dt.float32
F32R = mybir.dt.float32r
I32 = mybir.dt.int32
ALU = mybir.AluOpType
ACT = mybir.ActivationFunctionType
AX = mybir.AxisListType.X

P = 128
BLK = 512
EPS = 1e-5
SCAN_EPS = 1e-12
HIGH_BITS = -4096


def await_ge(eng, sem, value):
    eng.wait_ge(sem, value)
    if not isinstance(value, int):
        eng.nop(nofuse=True)


def high_part(dve, to, of):
    return dve.tensor_scalar(to.bitcast(I32), of.bitcast(I32), HIGH_BITS, None, ALU.bitwise_and)


def matmul_split(pe, out, lhs, rhs, start, stop):
    parts = ((0, 0), (0, 1), (1, 0))
    for i, (a, b) in enumerate(parts):
        ins = pe.matmul(out, lhs[a], rhs[b], start=start and i == 0,
                        stop=stop and i == len(parts) - 1, skip_group_check=True)
    return ins


class Steps:

    def __init__(self, eng, sem, start):
        self.eng, self.sem, self.n, self.start = eng, sem, 0, start

    def did(self, ins):
        ins.then_inc(self.sem, 1)
        self.n += 1

    def wait(self, back=0):
        await_ge(self.eng, self.sem, self.start + (self.n - back))


def build(nc, x, adj, gnn_w, gnn_b, w_rms1, w_rms2, w_in, conv_w, conv_b, w_x, w_dt, b_dt, a_log,
          d_skip, w_out, w_gate, w1, b1, w2, b2, out):
    L, D = x.shape
    DI = w_out.shape[0]
    NS = a_log.shape[1]
    DTR = w_dt.shape[0]
    NE = w_gate.shape[1]
    NT = L // P
    NB = L // BLK
    TB = BLK // P
    CD = D // P
    CI = DI // P
    XD = DTR + 2 * NS
    assert (CD, CI, TB, NB, NS, NE, XD) == (2, 4, 4, 4, 16, 8, 64)

    gnn_rows = nc.dram_tensor("gnn_rows", [L, D], F32, kind="Internal").ap()
    norm_rows = nc.dram_tensor("norm_rows", [L, D], F32, kind="Internal").ap()
    bc_rows = nc.dram_tensor("bc_rows", [2 * NS, L], F32, kind="Internal").ap()
    bc_pairs = bc_rows.rearrange("(a n) l -> n a l", a=2)
    adj_t = adj.rearrange("(t p) j -> t p j", p=P)

    ctx = ExitStack()
    with ctx:
        def sb(name, shape):
            return ctx.enter_context(nc.sbuf_tensor(name, shape, F32))

        def sem(name):
            return ctx.enter_context(nc.semaphore(name))

        with nc.sbuf_tensor("arena", [P, NB, NT, BLK], F32) as arena:
            pass
        U0, G0, D0, S0 = 0, CI, 2 * CI, 3 * CI
        parts = ctx.enter_context(nc.sbuf_tensor("parts", [P, NB * NT * BLK], F32R))
        with nc.sbuf_tensor("low", [P, 23056], F32) as low:
            pass
        low_parts = ctx.enter_context(nc.sbuf_tensor("low_parts", [P, 23056], F32R))

        def view(at, *dims, of=low):
            n = math.prod(dims)
            v = of[:, at:at + n]
            if len(dims) == 2:
                v = v.rearrange("p (a b) -> p a b", a=dims[0])
            elif len(dims) == 3:
                v = v.rearrange("p (a b c) -> p a b c", a=dims[0], b=dims[1])
            return v

        xrow = view(0, NT, D)
        z = view(4096, NT, D)
        wnat = view(19984, CD, D)
        ring = view(8192, 4, L)
        normed = view(8192, TB, D)
        pre = view(9216, TB, D)
        gT = view(10240, CD, BLK)
        preT = view(11264, CD, BLK)
        preT_lo = view(11264, CD, BLK, of=low_parts)
        preT_top = [view(at, BLK) for at in (15888, 19984)]
        preT_hi = [view(at, BLK, of=low_parts) for at in (15888, 19984)]
        stage = view(12288, CI, BLK + 4)
        xdbl = view(14352, BLK)
        win_sb = view(16400, CD, 2 * DI)
        win_top = [view(at, 2 * DI) for at in (14864, 20496)]
        win_hi = [view(at, 2 * DI, of=low_parts) for at in (14864, 20496)]
        win_lo = view(16400, CD, 2 * DI, of=low_parts)
        wT = view(18448, CD, D)
        gb_bc = view(18960, D)
        wx_sb = view(19216, CI, XD)
        wdt_sb = view(19472, DI)
        wout_sb = view(21520, CI, D)
        ones = view(22544, BLK)
        rsum = view(0, CI, BLK)
        bu = view(2048, 2, 2, BLK)
        bc = view(4096, 2, 2, BLK)
        gate = view(6144, 2, 2, BLK)
        gate_all = view(6144, CI, BLK)
        yc = view(8192, 2, 2, BLK)
        hT = view(10240, 2, CI, BLK)
        yg = view(10240, CI, BLK)
        gateT = view(12288, BLK)
        xmT = view(14336, CD, BLK)
        w1_sb = view(15360, 2, CD * DI)
        w2_sb = view(17408, 2, CI * D)
        acc = view(19456, TB, D)
        xm = view(20480, TB, D)

        w1_top = view(0, CD * DI)
        w2_top = view(1024, CI * D)
        hT_top = view(2048, CI, BLK)
        xmT_top = view(4096, CD, BLK)

        def part(at, *dims):
            v = parts[:, at:at + math.prod(dims)]
            if len(dims) == 2:
                return v.rearrange("p (a b) -> p a b", a=dims[0])
            return v.rearrange("p (a b c) -> p a b c", a=dims[0], b=dims[1])

        w1_hi, w1_lo, w2_hi, w2_lo = (part(2048 * i, 2, 1024) for i in range(4))
        hT_hi, hT_lo = (part(8192 + 4096 * i, 2, CI, BLK) for i in range(2))
        xmT_hi, xmT_lo = (part(16384 + 1024 * i, CD, BLK) for i in range(2))
        assert 16384 + 2048 <= 3 * NT * BLK and CD * DI == CI * D == 1024

        ident = sb("ident", [P, P])
        rowsum = sb("rowsum", [P, NT])
        deg = sb("deg", [P, NT])
        stats = sb("stats", [P, NT, 6])
        mv = sb("mv", [P, NT, 2])
        sa, sb_, sc_, sd_ = (sb(f"small{i}", [P, NT]) for i in range(4))
        zscale = sb("zscale", [P, NT])
        stats2 = sb("stats2", [P, TB, 6])
        mv2 = sb("mv2", [P, TB, 2])
        q = sb("q", [P, 2 * TB])
        qr = sb("qr", [P, 2 * TB])
        qt = sb("qt", [P, 2 * TB])
        VECS = 2 * CD + 3 * CI + NE * CI
        vec_rows = sb("vec_rows", [VECS, P])
        vecs = sb("vecs", [P, VECS])
        w1c, w2c = vecs[:, 0:CD], vecs[:, CD:2 * CD]
        cb, bdt, dp = (vecs[:, 2 * CD + i * CI:2 * CD + (i + 1) * CI] for i in range(3))
        B1 = 2 * CD + 3 * CI
        cw = sb("cw", [P, CI, 4])
        amat = sb("amat", [P, CI, NS])
        ahalf = sb("ahalf", [P, CI, NS])
        carry = sb("carry", [P, CI, NS])
        tot = sb("tot", [P, CI, NB])
        suffix = sb("suffix", [P, CI, NB])
        eps_c = sb("eps_c", [P, 1])
        halve_b = sb("halve_b", [XD, 1])
        wg_sb = sb("wg_sb", [P, CD, NE])
        b2_sb = sb("b2_sb", [NE, D])
        ss = sb("ss", [P, TB])
        ssv = sb("ssv", [P, TB])
        r2 = sb("r2", [P, TB])
        r2t = sb("r2t", [P, TB])
        gw = sb("gw", [P, TB, 1 + NE])
        gmax = sb("gmax", [P, TB])
        gsum = sb("gsum", [P, TB])

        ps = ctx.enter_context(nc.psum_tensor("ps", [P, 8, BLK], F32))

        consts_loaded = sem("consts_loaded")
        x_loaded = sem("x_loaded")
        adj_loaded = [sem(f"adj_loaded{i}") for i in range(4)]
        pool_made = sem("pool_made")
        w_turned = sem("w_turned")
        w_kept = sem("w_kept")
        diag_added = sem("diag_added")
        row_summed = sem("row_summed")
        adj_turned = sem("adj_turned")
        adj_kept = sem("adj_kept")
        dve_a = sem("dve_a")
        dve_z = sem("dve_z")
        act_a = sem("act_a")
        roots_a = sem("roots_a")
        z_made = sem("z_made")
        gcn_done = sem("gcn_done")
        gT_kept = sem("gT_kept")
        wmm_done = sem("wmm_done")
        q_made = sem("q_made")
        q_rooted = sem("q_rooted")
        dve_b = sem("dve_b")
        delta_made = sem("delta_made")
        pool_d = sem("pool_d")
        x1_made = sem("x1_made")
        pre_made = sem("pre_made")
        normed_made = sem("normed_made")
        pre_turned = sem("pre_turned")
        preT_kept = sem("preT_kept")
        pre_high = sem("pre_high")
        pre_split = sem("pre_split")
        pre_placed = sem("pre_placed")
        win_split = sem("win_split")
        win_high = sem("win_high")
        inproj_done = sem("inproj_done")
        inproj_used = sem("inproj_used")
        conv_done = sem("conv_done")
        u_made = sem("u_made")
        xdbl_done = sem("xdbl_done")
        xdbl_kept = sem("xdbl_kept")
        dt_done = sem("dt_done")
        act_soft = sem("act_soft")
        soft_made = sem("soft_made")
        dt_abs = sem("dt_abs")
        dt_relu = sem("dt_relu")
        rows_saved = sem("rows_saved")
        bc_saved = sem("bc_saved")
        phase_a = sem("phase_a")
        skip_made = sem("skip_made")
        r_made = sem("r_made")
        dve_r = sem("dve_r")
        dve_c = sem("dve_c")
        bc_loaded = [sem(f"bc_loaded{i}") for i in range(2)]
        bu_made = sem("bu_made")
        a_made = sem("a_made")
        gate_made = sem("gate_made")
        scanned = sem("scanned")
        carried = sem("carried")
        guarded = sem("guarded")
        lifted = sem("lifted")
        weighted = sem("weighted")
        pool_weighted = sem("pool_weighted")
        summed = sem("summed")
        y0_kept = sem("y0_kept")
        w1_loaded = [sem(f"w1_loaded{i}") for i in range(2)]
        w2_loaded = [sem(f"w2_loaded{i}") for i in range(2)]
        normed_loaded = sem("normed_loaded")
        gnn_loaded = sem("gnn_loaded")
        yg_made = sem("yg_made")
        mamba_done = sem("mamba_done")
        dve_p = sem("dve_p")
        v_made = sem("v_made")
        ss_made = sem("ss_made")
        ss_rooted = sem("ss_rooted")
        xm_made = sem("xm_made")
        xm_turned = sem("xm_turned")
        xmT_kept = sem("xmT_kept")
        gate_done = sem("gate_done")
        logit_made = sem("logit_made")
        gexp_made = sem("gexp_made")
        gw_made = sem("gw_made")
        gw_turned = sem("gw_turned")
        gateT_kept = sem("gateT_kept")
        hid_done = sem("hid_done")
        hid_read = sem("hid_read")
        hid_moved = sem("hid_moved")
        silu_made = sem("silu_made")
        x_split = sem("x_split")
        h_high = sem("h_high")
        h_split = sem("h_split")
        h_placed = sem("h_placed")
        w1_high = sem("w1_high")
        w1_split = sem("w1_split")
        w2_high = sem("w2_high")
        w2_split = sem("w2_split")
        w1_placed = sem("w1_placed")
        w2_placed = sem("w2_placed")
        exp_done = sem("exp_done")
        acc_made = sem("acc_made")
        acc_done = sem("acc_done")
        out_saved = sem("out_saved")

        block = ctx.enter_context(nc.Block())

        NP_CHUNK = NS * 2
        HEAD = 4
        BODY = 6
        STEPS = (NS - HEAD) // BODY
        SLOTS = 4
        assert (HEAD + STEPS * BODY, STEPS * SLOTS, BODY * 2) == (NS, NE, SLOTS * 3)
        NX = 2 + NE
        CONSTS = 16

        def xrow_block(k):
            return low[:, bass.ds(k * (TB * D), TB * D)].rearrange("p (t d) -> p t d", t=TB)

        @block.sync
        def _(sync):
            def const(to, of):
                sync.dma_start(to, of).then_inc(consts_loaded, 16)

            def load_adj(t, s, first):
                if not first:
                    await_ge(sync, row_summed, t - 3)
                    await_ge(sync, adj_turned, 4 * (t - 3))
                sync.dma_start(ring[:, s, :], adj_t[t, :, :]).then_inc(adj_loaded[s], 16)

            for s in range(2):
                load_adj(s, s, True)
            sync.dma_start(xrow, x.rearrange("(t p) d -> p t d", p=P)).then_inc(x_loaded, 16)
            for s in range(2, 4):
                load_adj(s, s, True)
            with sync.Fori(1, NT // 4) as it:
                for s in range(4):
                    load_adj(4 * it + s, s, False)
            const(wnat, gnn_w.rearrange("(a p) c -> p a c", p=P))
            at = 0
            for v in (w_rms1, w_rms2, conv_b, b_dt, d_skip, b1.rearrange("e n -> (e n)")):
                rows = v.shape[0] // P
                const(vec_rows[at:at + rows, :], v.rearrange("(a p) -> a p", p=P))
                at += rows
            const(gb_bc, gnn_b.partition_broadcast(P))
            const(win_sb, w_in.rearrange("(a p) n -> p a n", p=P))
            const(wx_sb, w_x.rearrange("(a p) n -> p a n", p=P))
            const(wdt_sb[0:DTR, :], w_dt)
            const(wout_sb, w_out.rearrange("(a p) n -> p a n", p=P))
            const(cw[:, :, :], conv_w.rearrange("(a p) o k -> p a (o k)", p=P))
            const(amat[:, :, :], a_log.rearrange("(a p) n -> p a n", p=P))
            const(wg_sb[:, :, :], w_gate.rearrange("(a p) n -> p a n", p=P))
            const(b2_sb[:, :], b2)

            def save(k):
                await_ge(sync, x1_made, k + 1)
                sync.dma_start(gnn_rows.rearrange("(k t p) d -> k p t d", p=P, t=TB)[k],
                               xrow_block(k)).then_inc(rows_saved, 16)
                await_ge(sync, normed_made, TB * (k + 1))
                sync.dma_start(norm_rows.rearrange("(k t p) d -> k p t d", p=P, t=TB)[k],
                               normed).then_inc(rows_saved, 16)
                await_ge(sync, xdbl_kept, k + 1)
                sync.dma_start(bc_rows.rearrange("n (k l) -> k n l", k=NB)[k],
                               xdbl[DTR:XD, :]).then_inc(bc_saved, 16)

            with sync.Fori(0, NB) as k:
                save(k)

            def load_bc(c, n, s, first):
                if not first:
                    await_ge(sync, bu_made, NP_CHUNK * c + 2 * (n - 1))
                    await_ge(sync, weighted, NP_CHUNK * c + 2 * (n - 1))
                    if isinstance(c, int) and (c == 0 or c == 1 and n < 2):
                        await_ge(sync, pool_weighted, NP_CHUNK * c + 2 * (n - 1))
                sync.dma_start(bc[:, s, :, :],
                               bc_rows.rearrange("(a n) (k l) -> k n a l", a=2, k=NB)[c, n]
                               .partition_broadcast(P)).then_inc(bc_loaded[s], 16)

            def load_rows(c):
                if not isinstance(c, int) or c > 0:
                    await_ge(sync, acc_made, TB * (NX * (c - 1) + 1))
                sync.dma_start(xm, norm_rows.rearrange("(k t p) d -> k p t d", p=P, t=TB)[c])\
                    .then_inc(normed_loaded, 16)

            def load_gnn(c):
                await_ge(sync, xm_turned, c + 1)
                sync.dma_start(xm, gnn_rows.rearrange("(k t p) d -> k p t d", p=P, t=TB)[c])\
                    .then_inc(gnn_loaded, 16)

            def store(c):
                await_ge(sync, acc_done, c + 1)
                sync.dma_start(out.rearrange("(k t p) d -> k p t d", p=P, t=TB)[c], acc)\
                    .then_inc(out_saved, 16)

            def head(c):
                for n in range(2):
                    load_bc(c, n, n, False)
                load_rows(c - 1)
                store(c - 2)
                for n in range(2, HEAD):
                    load_bc(c, n, n % 2, False)

            def rest(c):
                with sync.Fori(0, STEPS) as g:
                    for i in range(BODY):
                        load_bc(c, HEAD + BODY * g + i, i % 2, False)

            await_ge(sync, bc_saved, 16 * NB)
            await_ge(sync, gcn_done, 2 * NB)
            for n in range(2):
                load_bc(0, n, n, True)
            await_ge(sync, rows_saved, 32 * NB)
            sync.wait_ge(phase_a, 4)
            for n in range(2, HEAD):
                load_bc(0, n, n % 2, False)
            load_rows(0)
            rest(0)
            for n in range(HEAD):
                load_bc(1, n, n % 2, False)
            load_gnn(0)
            rest(1)
            with sync.Fori(2, NB) as c:
                head(c)
                load_gnn(c - 1)
                rest(c)
            load_rows(NB - 1)
            store(NB - 2)
            load_gnn(NB - 1)
            store(NB - 1)
            await_ge(sync, out_saved, 16 * NB)

        @block.gpsimd
        def _(pool):
            pool.memset(ident[:, :], 0.0).then_inc(pool_made, 1)
            pool.wait_ge(pool_made, 1)
            pool.affine_select(out=ident[:, :], in_=ident[:, :], compare_op=ALU.not_equal, fill=1.0,
                               base=0, pattern=[[-1, P]], channel_multiplier=1).then_inc(pool_made, 1)
            pool.memset(ones, 1.0).then_inc(pool_made, 1)
            pool.memset(eps_c[:, :], EPS).then_inc(pool_made, 1)
            pool.memset(halve_b[:, :], 1.0).then_inc(pool_made, 1)
            pool.memset(carry[:, :, :], 0.0).then_inc(pool_made, 1)
            pool.memset(gw[:, :, 0:1], 1.0).then_inc(pool_made, 1)
            pool.wait_ge(pool_made, 7)
            pool.memset(halve_b[DTR:DTR + NS, :], 0.5).then_inc(pool_made, 1)
            pool.wait_ge(pool_made, 8)

            def add_eye(t, s, loaded):
                await_ge(pool, adj_loaded[s], 16 * loaded)
                d = ring[:, s, bass.ds(t * P, P)]
                pool.tensor_tensor(d, d, ident[:, :], ALU.add).then_inc(diag_added, 1)

            for s in range(4):
                add_eye(s, s, 1)
            with pool.Fori(1, NT // 4) as it:
                for s in range(4):
                    add_eye(4 * it + s, s, it + 1)
            await_ge(pool, diag_added, NT)
            pool.nop().then_inc(phase_a, 1)

            def b_times(c, n, s, hf, first):
                pair = NP_CHUNK * c + 2 * n + hf
                if hf == 0:
                    await_ge(pool, bc_loaded[s], 16 * (c * (NS // 2) + (n - s) // 2 + 1))
                if not first:
                    await_ge(pool, scanned, 2 * (pair - 1))
                pool.tensor_tensor(bu[:, hf, :, :],
                                   arena[:, c, S0 + 2 * hf:S0 + 2 * hf + 2, :],
                                   bc[:, s, 0:1, :].broadcast_to([P, 2, BLK]), ALU.mult)\
                    .then_inc(bu_made, 1)

            def add_up(c, n, hf):
                pair = NP_CHUNK * c + 2 * n + hf
                await_ge(pool, weighted, pair + 1)
                y = arena[:, c, U0 + 2 * hf:U0 + 2 * hf + 2, :]
                pool.tensor_tensor(y, y, yc[:, hf, :, :], ALU.add).then_inc(summed, 1)

            def weigh_half(n, s, hf):
                pair = 2 * n + hf
                await_ge(pool, lifted, pair + 1)
                if not isinstance(pair, int) or pair >= 2:
                    await_ge(pool, summed, pair - 1)
                pool.tensor_tensor(yc[:, hf, 1, :], gate[:, hf, 1, :], bc[:, s, 1, :], ALU.mult)\
                    .then_inc(pool_weighted, 1)

            def chunk_0():
                def state(n, s, last):
                    for hf in range(2):
                        weigh_half(n, s, hf)
                        if not last:
                            b_times(0, n + 1, 1 - s, hf, False)

                await_ge(pool, rows_saved, 32 * NB)
                for hf in range(2):
                    b_times(0, 0, 0, hf, True)
                make_du(NB - 1)
                await_ge(pool, skip_made, 2 * NB)
                pool.wait_ge(phase_a, 4)
                for s in range(2):
                    state(s, s, False)
                with pool.Fori(1, NS // 2 - 1) as g:
                    for s in range(2):
                        state(2 * g + s, s, False)
                for s in range(2):
                    state(NS - 2 + s, s, s == 1)

            def chunk(c, after_0):
                for hf in range(2):
                    b_times(c, 0, 0, hf, False)
                    if not after_0:
                        add_up(c - 1, NS - 1, hf)
                b_times(c, 1, 1, 0, False)
                if after_0:
                    pool.wait_ge(y0_kept, 2)
                gate_y(c - 1)
                add_up(c, 0, 0)
                b_times(c, 1, 1, 1, False)
                add_up(c, 0, 1)
                for n in range(2, 4):
                    for hf in range(2):
                        b_times(c, n, n % 2, hf, False)
                        add_up(c, n - 1, hf)
                make_base(c - 1)
                with pool.Fori(1, NS // 4) as g:
                    for n in range(4):
                        for hf in range(2):
                            b_times(c, 4 * g + n, n % 2, hf, False)
                            add_up(c, 4 * g + n - 1, hf)

            def gate_y(c):
                await_ge(pool, summed, NP_CHUNK * (c + 1))
                for m in range(0, CI, 2):
                    pool.tensor_tensor(yg[:, m:m + 2, :], arena[:, c, U0 + m:U0 + m + 2, :],
                                       arena[:, c, G0 + m:G0 + m + 2, :], ALU.mult)\
                        .then_inc(yg_made, 1)

            def make_base(c):
                await_ge(pool, gnn_loaded, 16 * (c + 1))
                pool.tensor_tensor(acc, acc, xm, ALU.add).then_inc(acc_made, TB)

            def make_du(k):
                for m in range(0, CI, 2):
                    await_ge(pool, delta_made, CI * k + m + 2)
                    pool.tensor_tensor(arena[:, k, S0 + m:S0 + m + 2, :],
                                       arena[:, k, D0 + m:D0 + m + 2, :],
                                       arena[:, k, U0 + m:U0 + m + 2, :], ALU.mult).then_inc(pool_d, 1)
                await_ge(pool, xdbl_done, k + 1)
                await_ge(pool, pool_d, 2 * (k + 1))
                for m in range(0, CI, 2):
                    u = arena[:, k, U0 + m:U0 + m + 2, :]
                    pool.tensor_tensor(u, u, dp[:, m:m + 2].unsqueeze(2).broadcast_to([P, 2, BLK]),
                                       ALU.mult).then_inc(skip_made, 1)

            pool.wait_ge(w_kept, 2)
            make_du(0)
            with pool.Fori(1, NB - 1) as k:
                make_du(k)
            await_ge(pool, skip_made, 2 * (NB - 1))
            chunk_0()
            chunk(1, True)
            with pool.Fori(2, NB) as c:
                chunk(c, False)
            for hf in range(2):
                add_up(NB - 1, NS - 1, hf)
            def split_w1(e, s):
                await_ge(pool, w1_high, e + 1)
                pool.tensor_tensor(w1_lo[:, s, :], w1_sb[:, s, :], w1_top, ALU.subtract)\
                    .then_inc(w1_split, 1)

            def split_w2(e, s):
                await_ge(pool, w2_high, e + 1)
                pool.tensor_tensor(w2_lo[:, s, :], w2_sb[:, s, :], w2_top, ALU.subtract)\
                    .then_inc(w2_split, 1)

            split_w1(0, 0)
            make_base(NB - 1)
            with pool.Fori(0, NE // 2 - 1) as g:
                split_w1(2 * g + 1, 1)
                split_w2(2 * g, 0)
                split_w1(2 * g + 2, 0)
                split_w2(2 * g + 1, 1)
            split_w1(NE - 1, 1)
            split_w2(NE - 2, 0)
            split_w2(NE - 1, 1)

        @block.tensor
        def _(pe):
            pe.wait_ge(pool_made, 2)

            S_, W_, T_, I_ = 0, 2, 4, 6

            def turn_rows(t):
                pe.wait_ge(diag_added, t + 1)
                for b in range(4):
                    if t:
                        pe.wait_ge(adj_kept, 4 * (t - 1) + b + 1)
                    for j in range(4):
                        ins = pe.transpose(ps[:, 2 + b, j * P:(j + 1) * P],
                                           ring[:, t % 4, (4 * b + j) * P:(4 * b + j + 1) * P],
                                           ident[:, :])
                    ins.then_inc(adj_turned, 1)

            def gcn(k, c, lo=0, hi=NT):
                for j in range(lo, hi):
                    if isinstance(k, int) and k == 0:
                        pe.wait_ge(z_made, j + 1)
                    ins = pe.matmul(ps[:, S_ + c, :], z[:, j, c * P:(c + 1) * P], arena[:, k, j, :],
                                    start=(j == 0), stop=(j == NT - 1))
                if hi == NT:
                    ins.then_inc(gcn_done, 1)

            for t in range(NT):
                turn_rows(t)
                if t == 4:
                    pe.wait_ge(adj_kept, 4 * TB)
                if t > 4 and t % 4 >= 2:
                    lo = t - t % 4 - 4 + 2 * (t % 4 - 2)
                    for c in range(CD):
                        gcn(0, c, lo, lo + 2)
            gcn(0, 0, NT - 4)
            pe.wait_ge(adj_kept, 4 * NT)
            pe.wait_ge(consts_loaded, 16 * CONSTS)
            for a in range(CD):
                for c in range(CD):
                    pe.transpose(ps[:, 6, (c * CD + a) * P:(c * CD + a + 1) * P],
                                 wnat[:, a, c * P:(c + 1) * P], ident[:, :])
            pe.transpose(ps[:, 7, 0:VECS], vec_rows[:, :], ident[0:VECS, 0:VECS])\
                .then_inc(w_turned, 1)
            gcn(0, 1, NT - 4)
            pe.wait_ge(w_kept, 2)
            pe.wait_ge(win_split, 2 * CD)

            def in_proj(k, lo, hi):
                for m in range(lo, hi):
                    if m >= 2:
                        pe.wait_ge(inproj_used, 2 * CI * k + m - 1)
                    cols = slice(m * P, (m + 1) * P)
                    for c in range(CD):
                        ins = matmul_split(pe, ps[:, I_ + m % 2, :],
                                           (win_hi[c][:, cols], win_lo[:, c, cols]),
                                           (preT_hi[c], preT_lo[:, c, :]), c == 0, c == CD - 1)
                    ins.then_inc(inproj_done, 1)

            def block_a(k, first, last):
                for c in range(CD):
                    pe.wait_ge(gT_kept, 2 * k + c + 1)
                    for t in range(TB):
                        ins = pe.matmul(ps[:, W_ + t // 2, (t % 2) * D:(t % 2 + 1) * D],
                                        gT[:, c, t * P:(t + 1) * P], wT[:, c, :],
                                        start=(c == 0 and t % 2 == 0), stop=(c == CD - 1),
                                        skip_group_check=True)
                        if c == CD - 1:
                            ins.then_inc(wmm_done, 1)
                if not last:
                    gcn(k + 1, 0, 0, NT // 2)
                if not first:
                    pe.wait_ge(dt_relu, CI * k)
                    in_proj(k - 1, CI, 2 * CI)
                if not last:
                    gcn(k + 1, 0, NT // 2)
                for t in range(TB):
                    pe.wait_ge(pre_made, TB * k + t + 1)
                    if t == 0 and not first:
                        pe.wait_ge(dt_relu, CI * k)
                    for c in range(CD):
                        ins = pe.transpose(ps[:, T_ + c, t * P:(t + 1) * P],
                                           pre[:, t, c * P:(c + 1) * P], ident[:, :])
                ins.then_inc(pre_turned, 1)
                if not last:
                    gcn(k + 1, 1, 0, NT // 4)
                pe.wait_ge(pre_placed, CD * (k + 1))
                in_proj(k, 0, CI)
                if last:
                    in_proj(k, CI, 2 * CI)
                else:
                    gcn(k + 1, 1, NT // 4, 3 * NT // 4)
                for c in range(CI):
                    pe.wait_ge(u_made, CI * k + c + 1)
                    ins = pe.matmul(ps[0:XD, W_, :], wx_sb[:, c, :], arena[:, k, U0 + c, :],
                                    start=(c == 0), stop=(c == CI - 1))
                ins.then_inc(xdbl_done, 1)
                if not last:
                    gcn(k + 1, 1, 3 * NT // 4, 7 * NT // 8)
                pe.wait_ge(xdbl_kept, k + 1)
                for m in range(CI):
                    pe.matmul(ps[:, T_ + m, :], wdt_sb[0:DTR, m * P:(m + 1) * P], xdbl[0:DTR, :],
                              start=True, stop=True).then_inc(dt_done, 1)
                if not last:
                    gcn(k + 1, 1, 7 * NT // 8)

            block_a(0, True, False)
            with pe.Fori(1, NB - 1) as k:
                block_a(k, False, False)
            block_a(NB - 1, False, True)
            pe.wait_ge(dt_done, CI * NB)
            pe.nop().then_inc(phase_a, 1)
            pe.wait_ge(phase_a, 4)

            O_, M_ = 4, 6

            def prep(c, first, last):
                for m in range(CI):
                    if m % 2 == 0:
                        pe.wait_ge(yg_made, 2 * c + m // 2 + 1)
                    for t in range(TB):
                        if m == 0 and t % 2 == 0 and not first:
                            pe.wait_ge(acc_made, TB * (NX * c - 1) + t + 2)
                        ins = pe.matmul(ps[:, O_ + t // 2, (t % 2) * D:(t % 2 + 1) * D],
                                        yg[:, m, t * P:(t + 1) * P], wout_sb[:, m, :],
                                        start=(m == 0 and t % 2 == 0), stop=(m == CI - 1),
                                        skip_group_check=True)
                ins.then_inc(mamba_done, 1)
                for t in range(TB):
                    pe.wait_ge(xm_made, TB * c + t + 1)
                    if t == 0 and not first:
                        pe.wait_ge(silu_made, 3 * NE * c)
                    for a in range(CD):
                        ins = pe.transpose(ps[:, M_ + a, t * P:(t + 1) * P],
                                           xm[:, t, a * P:(a + 1) * P], ident[:, :])
                ins.then_inc(xm_turned, 1)
                pe.wait_ge(xmT_kept, 2 * (c + 1))
                for t in range(TB):
                    for a in range(CD):
                        ins = pe.matmul(ps[:, O_, t * NE:(t + 1) * NE], xmT[:, a, t * P:(t + 1) * P],
                                        wg_sb[:, a, :], start=(a == 0 and t == 0), stop=(a == CD - 1),
                                        skip_group_check=True)
                ins.then_inc(gate_done, 1)
                if last:
                    first_split(0, 0, 0)
                else:
                    first_layer(c, 0, 0, 0)
                pe.wait_ge(gw_made, c + 1)
                for t in range(TB):
                    ins = pe.transpose(ps[0:NE, O_ + 1, t * P:(t + 1) * P], gw[:, t, 1:], ident[:, :])
                ins.then_inc(gw_turned, 1)
                pe.wait_ge(gateT_kept, c + 1)
                for t in range(TB):
                    pe.matmul(ps[:, O_ + t // 2, (t % 2) * D:(t % 2 + 1) * D],
                              gateT[0:NE, t * P:(t + 1) * P], b2_sb[:, :],
                              start=(t % 2 == 0), stop=True, skip_group_check=True)\
                        .then_inc(exp_done, 1)

            def first_layer(c, e, s, half):
                count = NE * c + e
                if half == 0:
                    pe.wait_ge(w1_loaded[s], 16 * (c * (NE // 2) + (e - s) // 2 + 1))
                for m in range(2 * half, 2 * half + 2):
                    if half:
                        pe.wait_ge(hid_moved, 2 * count + m - 1)
                    elif isinstance(e, int) and e == 0:
                        pe.wait_ge(xmT_kept, 2 * (c + 1))
                    else:
                        pe.wait_ge(silu_made, 3 * (count - 1) + m + 1)
                    for a in range(CD):
                        ins = pe.matmul(ps[:, M_ + m % 2, :],
                                        w1_sb[:, s, a * DI + m * P:a * DI + (m + 1) * P],
                                        xmT[:, a, :], start=(a == 0), stop=(a == CD - 1))
                    ins.then_inc(hid_done, 1)

            def second_layer(c, e, s, half):
                if half == 0:
                    pe.wait_ge(silu_made, 3 * (NE * c + e + 1))
                    pe.wait_ge(w2_loaded[s], 16 * (c * (NE // 2) + (e - s) // 2 + 1))
                pe.wait_ge(acc_made, TB * (NX * c + 1 + e) + 2 * half + 2)
                for t in range(2 * half, 2 * half + 2):
                    for m in range(CI):
                        ins = pe.matmul(ps[:, O_ + half, (t % 2) * D:(t % 2 + 1) * D],
                                        hT[:, s, m, t * P:(t + 1) * P], w2_sb[:, s, m * D:(m + 1) * D],
                                        start=(m == 0 and t % 2 == 0), stop=(m == CI - 1),
                                        skip_group_check=True)
                    ins.then_inc(exp_done, 1)

            def layers(c, e, s):
                first_layer(c, e, s, 0)
                second_layer(c, e - 1, 1 - s, 0)
                first_layer(c, e, s, 1)
                second_layer(c, e - 1, 1 - s, 1)

            def experts(c):
                first_layer(c, 0, 0, 1)
                layers(c, 1, 1)
                with pe.Fori(1, NE // 2) as g:
                    for s in range(2):
                        layers(c, 2 * g + s, s)
                for half in range(2):
                    second_layer(c, NE - 1, 1, half)

            def sum_y(n, first, last):
                for hf in range(2):
                    pair = 2 * n + hf
                    pe.wait_ge(weighted, pair + 1)
                    pe.wait_ge(pool_weighted, pair + 1)
                    for j in range(2):
                        ins = pe.matmul(ps[:, 4 + 2 * hf + j, :], ident[:, :], yc[:, hf, j, :],
                                        start=first, stop=last)
                    ins.then_inc(summed, 1)

            sum_y(0, True, False)
            with pe.Fori(1, NS - 1) as n:
                sum_y(n, False, False)
            sum_y(NS - 1, False, True)
            SILU_0 = 3 * NE * (NB - 1)

            def first_split(e, s, half):
                count = NE * (NB - 1) + e
                if half == 0:
                    pe.wait_ge(w1_split, e + 1)
                    pe.wait_ge(w1_placed, e + 1)
                for m in range(2 * half, 2 * half + 2):
                    if m == 2:
                        pe.wait_ge(hid_read, e + 1)
                    elif m == 3:
                        pe.wait_ge(silu_made, SILU_0 + 4 * e + 1)
                    elif isinstance(e, int) and e == 0:
                        pe.wait_ge(x_split, 1)
                        pe.wait_ge(h_placed, CD)
                    else:
                        pe.wait_ge(silu_made, SILU_0 + 4 * (e - 1) + 3 + m)
                    for a in range(CD):
                        cols = slice(a * DI + m * P, a * DI + (m + 1) * P)
                        ins = matmul_split(pe, ps[:, M_ + m % 2, :],
                                           (w1_hi[:, s, cols], w1_lo[:, s, cols]),
                                           (xmT_hi[:, a, :], xmT_lo[:, a, :]),
                                           a == 0, a == CD - 1)
                    ins.then_inc(hid_done, 1)

            def second_split(e, s, half):
                if half == 0:
                    pe.wait_ge(h_split, 2 * (e + 1))
                    pe.wait_ge(h_placed, CD + 2 * (e + 1))
                    pe.wait_ge(w2_split, e + 1)
                    pe.wait_ge(w2_placed, e + 1)
                pe.wait_ge(acc_made, TB * (NX * (NB - 1) + 1 + e) + 2 * half + 2)
                for t in range(2 * half, 2 * half + 2):
                    rows = slice(t * P, (t + 1) * P)
                    for m in range(CI):
                        cols = slice(m * D, (m + 1) * D)
                        ins = matmul_split(pe, ps[:, O_ + half, (t % 2) * D:(t % 2 + 1) * D],
                                           (hT_hi[:, s, m, rows], hT_lo[:, s, m, rows]),
                                           (w2_hi[:, s, cols], w2_lo[:, s, cols]),
                                           m == 0 and t % 2 == 0, m == CI - 1)
                    ins.then_inc(exp_done, 1)

            def split_layers(e, s):
                first_split(e, s, 0)
                second_split(e - 1, 1 - s, 0)
                first_split(e, s, 1)
                second_split(e - 1, 1 - s, 1)

            prep(0, True, False)
            experts(0)
            with pe.Fori(1, NB - 1) as c:
                prep(c, False, False)
                experts(c)
            prep(NB - 1, False, True)
            first_split(0, 0, 1)
            split_layers(1, 1)
            with pe.Fori(1, NE // 2) as g:
                for s in range(2):
                    split_layers(2 * g + s, s)
            for half in range(2):
                second_split(NE - 1, 1, half)

        @block.scalar
        def _(act):
            def keep_rows(t, s):
                blk = (t - s) // 4 if isinstance(t, int) else t_block
                for b in range(4):
                    await_ge(act, adj_turned, 4 * t + b + 1)
                    act.activation(arena[:, blk, 4 * b:4 * b + 4, s * P:(s + 1) * P],
                                   ps[:, 2 + b, :].rearrange("p (j i) -> p j i", j=4),
                                   ACT.Copy).then_inc(adj_kept, 1)

            t_block = 0
            for s in range(4):
                keep_rows(s, s)
            act.wait_ge(pool_made, 8)
            act.wait_ge(dve_a, 1)
            act.activation(sb_[:, :], mv[:, :, 1], ACT.Sqrt, bias=eps_c[:, :]).then_inc(roots_a, 1)

            def degree_roots(b):
                await_ge(act, row_summed, 4 * (b + 1))
                act.activation(sa[:, bass.ds(4 * b, 4)], rowsum[:, bass.ds(4 * b, 4)], ACT.Sqrt)\
                    .then_inc(roots_a, 1)

            degree_roots(0)
            with act.Fori(1, NT // 4) as it:
                t_block = it
                for s in range(4):
                    keep_rows(4 * it + s, s)
                degree_roots(it)
            act.wait_ge(w_turned, 1)
            act.activation(wT, ps[:, 6, :].rearrange("p (a n) -> p a n", a=CD), ACT.Copy)\
                .then_inc(w_kept, 1)
            act.activation(vecs[:, :], ps[:, 7, 0:VECS], ACT.Copy).then_inc(w_kept, 1)
            await_ge(act, consts_loaded, 16 * CONSTS)
            act.activation(amat[:, :, :], amat[:, :, :], ACT.Exp).then_inc(act_a, 1)
            act.wait_ge(act_a, 1)
            act.activation(ahalf[:, :, :], amat[:, :, :], ACT.Copy, scale=-0.5).then_inc(act_a, 1)
            act.wait_ge(act_a, 2)
            act.activation(amat[:, :, :], amat[:, :, :], ACT.Copy, scale=-1.0).then_inc(act_a, 1)

            S_, W_, T_, I_ = 0, 2, 4, 6

            def softplus(k):
                for m in range(CI):
                    await_ge(act, dt_done, CI * k + m + 1)
                    act.activation(arena[:, k, D0 + m, :], ps[:, T_ + m, :], ACT.Abs,
                                   bias=bdt[:, m:m + 1]).then_inc(dt_abs, 1)

            def softplus_rest(k):
                dl = arena[:, k, D0:D0 + CI, :]
                await_ge(act, dt_abs, CI * (k + 1))
                act.activation(dl, dl, ACT.Exp, scale=-1.0).then_inc(act_soft, 1)
                await_ge(act, act_soft, k + 1)
                act.activation(dl, dl, ACT.Ln, bias=1.0).then_inc(soft_made, 1)

            def gate_silu(k):
                for m in range(CI):
                    await_ge(act, inproj_done, 2 * CI * k + CI + m + 1)
                    act.activation(arena[:, k, G0 + m, :], ps[:, I_ + m % 2, :], ACT.Silu)\
                        .then_inc(inproj_used, 1)

            def block_a(k, first, last):
                if not first:
                    softplus(k - 1)
                await_ge(act, gcn_done, 2 * k + 1)
                if not first:
                    await_ge(act, wmm_done, TB * k)
                act.activation(gT[:, 0, :], ps[:, S_, :], ACT.Copy).then_inc(gT_kept, 1)
                if not first:
                    softplus_rest(k - 1)
                await_ge(act, q_made, k + 1)
                act.activation(qr[:, :], q[:, :], ACT.Sqrt).then_inc(q_rooted, 1)
                if not first:
                    gate_silu(k - 1)
                await_ge(act, pre_turned, k + 1)
                act.activation(preT[:, 0, :], ps[:, T_, :], ACT.Copy, scale=w1c[:, 0:1])\
                    .then_inc(preT_kept, 1)
                await_ge(act, pre_split, CD * (k + 1))
                for c in range(CD):
                    act.activation(preT_hi[c], preT_top[c], ACT.Copy).then_inc(pre_placed, 1)
                for m in range(CI):
                    await_ge(act, inproj_done, 2 * CI * k + m + 1)
                    if m == 0 and not first:
                        await_ge(act, conv_done, (CI + 1) * k + 1)
                    act.activation(stage[:, m, 3:3 + BLK], ps[:, I_ + m % 2, :], ACT.Copy)
                    act.activation(arena[:, k, U0 + m, :], ps[:, I_ + m % 2, :], ACT.Copy,
                                   scale=cw[:, m, 3:4]).then_inc(inproj_used, 1)
                if last:
                    gate_silu(k)
                for m in range(CI):
                    await_ge(act, conv_done, (CI + 1) * k + m + 2)
                    act.activation(arena[:, k, U0 + m, :], arena[:, k, U0 + m, :], ACT.Silu,
                                   bias=cb[:, m:m + 1]).then_inc(u_made, 1)
                await_ge(act, xdbl_done, k + 1)
                if not first:
                    await_ge(act, bc_saved, 16 * k)
                act.activation(xdbl[0:XD, :], ps[0:XD, W_, :], ACT.Copy, scale=halve_b[:, :]).then_inc(xdbl_kept, 1)

            block_a(0, True, False)
            with act.Fori(1, NB - 1) as k:
                block_a(k, False, False)
            block_a(NB - 1, False, True)
            softplus(NB - 1)
            softplus_rest(NB - 1)
            await_ge(act, soft_made, NB)
            await_ge(act, xdbl_kept, NB)
            act.nop().then_inc(phase_a, 1)
            act.wait_ge(act_a, 3)

            def load_w1(e, s):
                act.dma_start(w1_sb[:, s, :].rearrange("p (a n) -> p a n", a=CD),
                              w1.rearrange("e (a p) n -> e p a n", p=P)[e]).then_inc(w1_loaded[s], 16)

            def load_w2(e, s):
                act.dma_start(w2_sb[:, s, :].rearrange("p (a n) -> p a n", a=CI),
                              w2.rearrange("e (a p) n -> e p a n", p=P)[e]).then_inc(w2_loaded[s], 16)

            def decay(c, n, hf, first):
                pair = NP_CHUNK * c + 2 * n + hf
                if not first:
                    await_ge(act, weighted, pair - 1)
                    if isinstance(c, int) and c == 0:
                        await_ge(act, pool_weighted, pair - 1)
                for m in range(2 * hf, 2 * hf + 2):
                    act.activation(ps[:, m, :], arena[:, c, D0 + m, :], ACT.Exp,
                                   scale=amat[:, m, bass.ds(n, 1)]).then_inc(a_made, 1)

            def tanh(c, n, hf):
                for m in range(2 * hf, 2 * hf + 2):
                    act.activation(gate[:, hf, m % 2, :], rsum[:, m, :], ACT.Tanh,
                                   scale=ahalf[:, m, bass.ds(n, 1)], bias=-0.5 * math.log(SCAN_EPS))\
                        .then_inc(gate_made, 1)

            def hidden(c, e, s):
                count = NE * c + e
                for m in range(2, CI):
                    await_ge(act, hid_done, CI * count + m + 1)
                    act.activation(hT[:, s, m, :], ps[:, 6 + m % 2, :], ACT.Silu,
                                   bias=vecs[:, bass.ds(B1 + CI * e + m, 1)]).then_inc(silu_made, 1)
                await_ge(act, hid_moved, 2 * count + 2)
                act.activation(hT[:, s, 0:2, :], hT[:, s, 0:2, :], ACT.Silu).then_inc(silu_made, 1)

            def start_expert(c, e, s):
                await_ge(act, hid_done, CI * (NE * c + e) + 2)
                load_w2(e, s)
                for m in range(2):
                    act.activation(hT[:, s, m, :], ps[:, 6 + m, :], ACT.Identity,
                                   bias=vecs[:, bass.ds(B1 + CI * e + m, 1)]).then_inc(hid_moved, 1)

            def squares(c):
                await_ge(act, v_made, c + 1)
                for t in range(TB):
                    act.activation(yg[:, t, 0:D], acc[:, t, :], ACT.Square, accum_out=ss[:, t:t + 1])\
                        .then_inc(ss_made, 1)
                await_ge(act, ss_made, TB * (c + 1))
                act.activation(r2[:, :], ss[:, :], ACT.Sqrt, scale=1.0 / D, bias=eps_c[:, :])\
                    .then_inc(ss_rooted, 1)

            def keep_xmT(c):
                await_ge(act, xm_turned, c + 1)
                act.activation(xmT[:, 0, :], ps[:, 6, :], ACT.Copy, scale=w2c[:, 0:1])\
                    .then_inc(xmT_kept, 1)

            def gate_exp(c):
                await_ge(act, logit_made, c + 1)
                act.activation(gw[:, :, 1:], gw[:, :, 1:], ACT.Exp).then_inc(gexp_made, 1)

            def chunk(c, first_chunk):
                if first_chunk:
                    act.wait_ge(delta_made, CI)
                else:
                    act.wait_ge(pool_weighted, NP_CHUNK)
                for hf in range(2):
                    decay(c, 0, hf, first_chunk)
                if first_chunk:
                    act.wait_ge(phase_a, 4)
                for q in range(2 * HEAD):
                    if q < 2:
                        await_ge(act, r_made, 2 * c + q + 1)
                    else:
                        decay(c, q // 2, q % 2, False)
                    tanh(c, q // 2, q % 2)
                    if not first_chunk:
                        if q == 4:
                            squares(c - 1)
                        elif q == 6:
                            keep_xmT(c - 1)
                        elif q == 7:
                            gate_exp(c - 1)
                with act.Fori(0, STEPS) as g:
                    for q in range(2 * BODY):
                        decay(c, HEAD + BODY * g + q // 2, q % 2, False)
                        tanh(c, HEAD + BODY * g + q // 2, q % 2)
                        if first_chunk:
                            continue
                        i = q // 3
                        e = SLOTS * g + i
                        if q % 3 == 0:
                            start_expert(c - 1, e, i % 2)
                        elif q % 3 == 2:
                            hidden(c - 1, e, i % 2)
                            load_w1(e + 2 if i < 2 else SLOTS * (STEPS - 1 - g) + i - 2, i % 2)

            chunk(0, True)
            for s in range(2):
                load_w1(s, s)
            with act.Fori(1, NB) as c:
                chunk(c, False)
            c = NB - 1
            squares(c)
            keep_xmT(c)
            await_ge(act, h_high, 1)
            for a in range(CD):
                act.activation(xmT_hi[:, a, :], xmT_top[:, a, :], ACT.Copy).then_inc(h_placed, 1)
            gate_exp(c)

            def place_hidden(e, s, half):
                await_ge(act, h_high, 2 * e + half + 2)
                m = 2 * half
                act.activation(hT_hi[:, s, m:m + 2, :], hT_top[:, m:m + 2, :], ACT.Copy)\
                    .then_inc(h_placed, 1)

            def expert(e, s, more):
                count = NE * c + e

                def silu(m):
                    act.activation(hT[:, s, m, :], ps[:, 6 + m % 2, :], ACT.Silu,
                                   bias=vecs[:, bass.ds(B1 + CI * e + m, 1)]).then_inc(silu_made, 1)

                await_ge(act, hid_done, CI * count + 2)
                load_w2(e, s)
                silu(1)
                await_ge(act, hid_read, e + 1)
                act.activation(hT[:, s, 0, :], hT[:, s, 0, :], ACT.Silu).then_inc(silu_made, 1)
                place_hidden(e, s, 0)
                for m in (2, 3):
                    await_ge(act, hid_done, CI * count + m + 1)
                    silu(m)
                place_hidden(e, s, 1)
                if more:
                    load_w1(e + 2, s)

            with act.Fori(0, NE // 2 - 1) as g:
                for s in range(2):
                    expert(2 * g + s, s, True)
            for s in range(2):
                expert(NE - 2 + s, s, False)

        @block.vector
        def _(dve):
            def newton(st, y, v, tmp):
                st.did(dve.tensor_tensor(tmp, y, y, ALU.mult))
                st.wait()
                st.did(dve.tensor_tensor(tmp, tmp, v, ALU.mult))
                st.wait()
                st.did(dve.tensor_scalar(tmp, tmp, -0.5, 1.5, ALU.mult, ALU.add))
                st.wait()
                st.did(dve.tensor_tensor(y, y, tmp, ALU.mult))
                st.wait()

            def sum_rows(t, s):
                await_ge(dve, diag_added, t + 1)
                dve.tensor_reduce(rowsum[:, bass.ds(t, 1)], ring[:, s, :], AX, ALU.add)\
                    .then_inc(row_summed, 1)

            def x_stats(lo, hi):
                for t in range(lo, hi):
                    dve.bn_stats(stats[:, t, :], xrow[:, t, :]).then_inc(dve_r, 1)

            sum_rows(0, 0)
            sum_rows(1, 1)
            dve.wait_ge(x_loaded, 16)
            x_stats(0, NT // 2)
            sum_rows(2, 2)
            x_stats(NT // 2, NT)
            sum_rows(3, 3)
            await_ge(dve, dve_r, NT)
            for t in range(NT):
                ins = dve.bn_aggr(mv[:, t, :], stats[:, t, :])
            ins.then_inc(dve_a, 1)
            a = Steps(dve, dve_a, 0)
            a.n = 1
            a.wait()
            a.did(dve.tensor_scalar(sd_[:, :], mv[:, :, 1], EPS, None, ALU.add))
            dve.wait_ge(roots_a, 1)
            a.did(dve.reciprocal(zscale[:, :], sb_[:, :]))
            a.wait()
            newton(a, zscale[:, :], sd_[:, :], sc_[:, :])

            def make_z(b):
                st = Steps(dve, dve_z, b * STEPS_Z)
                four = bass.ds(4 * b, 4)
                await_ge(dve, row_summed, 4 * (b + 1))
                await_ge(dve, roots_a, b + 2)
                st.did(dve.reciprocal(deg[:, four], sa[:, four]))
                st.wait()
                newton(st, deg[:, four], rowsum[:, four], sc_[:, four])
                st.did(dve.tensor_tensor(zscale[:, four], zscale[:, four], deg[:, four], ALU.mult))
                st.wait()
                to = low[:, bass.ds(4096 + 4 * D * b, 4 * D)].rearrange("p (t d) -> p t d", t=4)
                of = low[:, bass.ds(4 * D * b, 4 * D)].rearrange("p (t d) -> p t d", t=4)
                for t in range(4):
                    dve.tensor_scalar(to[:, t, :], of[:, t, :], mv[:, bass.ds(4 * b + t, 1), 0],
                                      zscale[:, bass.ds(4 * b + t, 1)], ALU.subtract, ALU.mult)\
                        .then_inc(z_made, 1)
                return st.n

            STEPS_Z = 6
            with dve.Fori(1, NT // 4) as it:
                for s in range(2):
                    sum_rows(4 * it + s, s)
                assert make_z(it - 1) == STEPS_Z
                for s in range(2, 4):
                    sum_rows(4 * it + s, s)
            make_z(NT // 4 - 1)
            dve.memset(stage[:, :, 0:3], 0.0).then_inc(conv_done, 1)
            dve.wait_ge(consts_loaded, 16 * CONSTS)
            for c in range(CD):
                high_part(dve, win_top[c], win_sb[:, c, :]).then_inc(win_high, 1)
            dve.wait_ge(win_high, CD)
            for c in range(CD):
                dve.tensor_tensor(win_lo[:, c, :], win_sb[:, c, :], win_top[c], ALU.subtract)\
                    .then_inc(win_split, 1)
            dve.wait_ge(win_split, CD)
            for c in range(CD):
                dve.tensor_copy(win_hi[c], win_top[c]).then_inc(win_split, 1)

            S_, W_, T_, I_ = 0, 2, 4, 6

            def relu(k):
                for m in range(CI):
                    await_ge(dve, dt_done, CI * k + m + 1)
                    await_ge(dve, dt_abs, CI * k + m + 1)
                    dve.tensor_scalar(arena[:, k, S0 + m, :], ps[:, T_ + m, :], bdt[:, m:m + 1], 0.0,
                                      ALU.add, ALU.max).then_inc(dt_relu, 1)

            def make_delta(k):
                await_ge(dve, soft_made, k + 1)
                await_ge(dve, dt_relu, CI * (k + 1))
                for m in range(CI):
                    d = arena[:, k, D0 + m, :]
                    dve.scalar_tensor_tensor(d, arena[:, k, S0 + m, :], 1.0, d, ALU.mult, ALU.add,
                                             accum_out=tot[:, m, bass.ds(k, 1)])\
                        .then_inc(delta_made, 1)

            def block_a(k, first):
                st = Steps(dve, dve_b, k * STEPS_A)
                if not first:
                    relu(k - 1)
                await_ge(dve, gcn_done, 2 * k + 2)
                await_ge(dve, gT_kept, 2 * k + 1)
                if not first:
                    await_ge(dve, wmm_done, TB * k)
                dve.tensor_copy(gT[:, 1, :], ps[:, S_ + 1, :]).then_inc(gT_kept, 1)
                if not first:
                    await_ge(dve, rows_saved, 32 * k)
                xb = xrow_block(k)
                for t in range(TB):
                    await_ge(dve, wmm_done, TB * k + 2 * (t // 2) + 2)
                    st.did(dve.scalar_tensor_tensor(
                        normed[:, t, :], ps[:, W_ + t // 2, (t % 2) * D:(t % 2 + 1) * D],
                        deg[:, bass.ds(TB * k + t, 1)], gb_bc, ALU.mult, ALU.add))
                for t in range(TB):
                    st.wait(TB - 1)
                    st.did(dve.scalar_tensor_tensor(
                        xb[:, t, :], normed[:, t, :], 0.0, xb[:, t, :], ALU.max, ALU.add))
                for t in range(TB):
                    st.wait(TB - 1)
                    st.did(dve.bn_stats(stats2[:, t, :], xb[:, t, :]))
                for t in range(TB):
                    st.wait(TB - 1)
                    st.did(dve.bn_aggr(mv2[:, t, :], stats2[:, t, :]))
                st.wait()
                st.did(dve.tensor_scalar(q[:, 0:TB], mv2[:, :, 1], EPS, None, ALU.add))
                st.wait()
                dve.scalar_tensor_tensor(q[:, TB:], q[:, 0:TB], EPS, mv2[:, :, 1], ALU.mult, ALU.add)\
                    .then_inc(q_made, 1)
                await_ge(dve, q_made, k + 1)
                dve.nop().then_inc(x1_made, 1)
                await_ge(dve, q_rooted, k + 1)
                st.did(dve.reciprocal(qr[:, :], qr[:, :]))
                st.wait()
                newton(st, qr[:, :], q[:, :], qt[:, :])
                for t in range(TB):
                    dve.tensor_scalar(pre[:, t, :], xb[:, t, :], mv2[:, t, 0:1],
                                      qr[:, TB + t:TB + t + 1], ALU.subtract, ALU.mult)\
                        .then_inc(pre_made, 1)
                for t in range(TB):
                    dve.tensor_scalar(normed[:, t, :], xb[:, t, :], mv2[:, t, 0:1], qr[:, t:t + 1],
                                      ALU.subtract, ALU.mult).then_inc(normed_made, 1)
                await_ge(dve, pre_turned, k + 1)
                dve.tensor_scalar(preT[:, 1, :], ps[:, T_ + 1, :], w1c[:, 1:2], None, ALU.mult)\
                    .then_inc(preT_kept, 1)
                await_ge(dve, preT_kept, 2 * (k + 1))
                for c in range(CD):
                    high_part(dve, preT_top[c], preT[:, c, :]).then_inc(pre_high, 1)
                for c in range(CD):
                    await_ge(dve, pre_high, CD * k + c + 1)
                    dve.tensor_tensor(preT_lo[:, c, :], preT[:, c, :], preT_top[c], ALU.subtract)\
                        .then_inc(pre_split, 1)
                for m0 in range(0, CI, 2):
                    for j in range(3):
                        for m in (m0, m0 + 1):
                            if j == 0:
                                await_ge(dve, inproj_used, 2 * CI * k + m + 1)
                            else:
                                st.wait(0 if j == 2 and m > m0 else 1)
                            o = arena[:, k, U0 + m, :]
                            ins = dve.scalar_tensor_tensor(o, stage[:, m, j:j + BLK],
                                                           cw[:, m, j:j + 1], o, ALU.mult, ALU.add)
                            if j < 2:
                                st.did(ins)
                            else:
                                ins.then_inc(conv_done, 1)
                await_ge(dve, conv_done, (CI + 1) * k + CI + 1)
                dve.tensor_copy(stage[:, :, 0:3], stage[:, :, BLK:BLK + 3]).then_inc(conv_done, 1)
                if not first:
                    make_delta(k - 1)
                return st.n

            STEPS_A = 4 * TB + 1 + 1 + 4 + 2 * CI
            assert block_a(0, True) == STEPS_A
            with dve.Fori(1, NB) as k:
                block_a(k, False)
            relu(NB - 1)
            make_delta(NB - 1)
            await_ge(dve, delta_made, CI * NB)
            st = Steps(dve, dve_b, NB * STEPS_A)
            st.did(dve.memset(suffix[:, :, NB - 1], 0.0))
            for k in range(NB - 2, -1, -1):
                st.wait()
                st.did(dve.tensor_tensor(suffix[:, :, k], suffix[:, :, k + 1], tot[:, :, k + 1],
                                         ALU.add))
            st.wait()
            dve.nop().then_inc(phase_a, 1)
            dve.wait_ge(phase_a, 4)

            def make_r(c):
                dve.tensor_copy(gate_all, arena[:, c, D0:D0 + CI, :]).then_inc(dve_c, 1)
                dve.tensor_copy(rsum[:, :, BLK - 1:BLK], suffix[:, :, bass.ds(c, 1)])
                await_ge(dve, dve_c, c + 1)
                for m in range(CI):
                    ins = dve.tensor_tensor_scan(
                        rsum[:, m, 0:BLK - 1][:, ::-1], ones[:, 0:BLK - 1],
                        gate_all[:, m, 1:BLK][:, ::-1], suffix[:, m, bass.ds(c, 1)],
                        ALU.mult, ALU.add)
                    if m % 2:
                        ins.then_inc(r_made, 1)

            def scan(c, n, s, hf, j, first_chunk):
                pair = NP_CHUNK * c + 2 * n + hf
                if j == 0:
                    if hf == 0:
                        await_ge(dve, bc_loaded[s], 16 * (c * (NS // 2) + (n - s) // 2 + 1))
                        if not first_chunk:
                            await_ge(dve, carried, NP_CHUNK * (c - 1) + 2 * n + 2)
                    await_ge(dve, bu_made, pair + 1)
                m = 2 * hf + j
                await_ge(dve, a_made, 2 * pair + j + 1)
                dve.tensor_tensor_scan(ps[:, m, :], ps[:, m, :], bu[:, hf, j, :],
                                       carry[:, m, bass.ds(n, 1)], ALU.mult, ALU.add)\
                    .then_inc(scanned, 1)

            def scans(c, n, s, hf, first_chunk):
                for j in range(2):
                    scan(c, n, s, hf, j, first_chunk)

            def keep_carry(c, n, hf):
                pair = NP_CHUNK * c + 2 * n + hf
                await_ge(dve, gate_made, 2 * pair + 2)
                await_ge(dve, scanned, 2 * pair + 2)
                dve.tensor_copy(carry[:, 2 * hf:2 * hf + 2, bass.ds(n, 1)],
                                ps[:, 2 * hf:2 * hf + 2, BLK - 1:BLK]).then_inc(carried, 1)

            def guard(c, n, hf):
                pair = NP_CHUNK * c + 2 * n + hf
                h = ps[:, 2 * hf:2 * hf + 2, :]
                await_ge(dve, carried, pair + 1)
                if isinstance(c, int) and c == 0:
                    dve.scalar_tensor_tensor(gate[:, hf, 1, :], gate[:, hf, 1, :], 1.0, h[:, 1, :],
                                             ALU.add, ALU.mult).then_inc(lifted, 1)
                    dve.scalar_tensor_tensor(h[:, 0, :], gate[:, hf, 0, :], 1.0, h[:, 0, :],
                                             ALU.add, ALU.mult).then_inc(guarded, 1)
                else:
                    dve.scalar_tensor_tensor(h, gate[:, hf, :, :], 1.0, h, ALU.add, ALU.mult)\
                        .then_inc(guarded, 1)

            def weigh(c, n, s, hf, first, tiles):
                pair = NP_CHUNK * c + 2 * n + hf
                await_ge(dve, guarded, pair + 1)
                if not first:
                    await_ge(dve, summed, pair - 1)
                dve.tensor_tensor(yc[:, hf, 0:tiles, :], ps[:, 2 * hf:2 * hf + tiles, :],
                                  bc[:, s, 1:2, :].broadcast_to([P, tiles, BLK]), ALU.mult)\
                    .then_inc(weighted, 1)

            def add_norm(c, stored):
                await_ge(dve, normed_loaded, 16 * (c + 1))
                await_ge(dve, mamba_done, c + 1)
                if stored:
                    await_ge(dve, out_saved, 16 * c)
                o = ps[:, 4:6, :].rearrange("p a (b d) -> p (a b) d", b=2)
                dve.tensor_tensor(acc, o, xm, ALU.add).then_inc(v_made, 1)

            def rms_norm(c):
                st = Steps(dve, dve_p, c * STEPS_P)
                await_ge(dve, ss_made, TB * (c + 1))
                st.did(dve.tensor_scalar(ssv[:, :], ss[:, :], 1.0 / D, EPS, ALU.mult, ALU.add))
                await_ge(dve, ss_rooted, c + 1)
                st.did(dve.reciprocal(r2[:, :], r2[:, :]))
                st.wait()
                newton(st, r2[:, :], ssv[:, :], r2t[:, :])
                await_ge(dve, v_made, c + 1)
                for t in range(TB):
                    dve.tensor_scalar(xm[:, t, :], acc[:, t, :], r2[:, t:t + 1], None, ALU.mult)\
                        .then_inc(xm_made, 1)
                return st.n

            def keep_xmT(c):
                await_ge(dve, xm_turned, c + 1)
                dve.tensor_scalar(xmT[:, 1, :], ps[:, 7, :], w2c[:, 1:2], None, ALU.mult)\
                    .then_inc(xmT_kept, 1)

            def gate_logits(c, at):
                st = Steps(dve, dve_p, c * STEPS_P)
                st.n = at
                await_ge(dve, gate_done, c + 1)
                lg = ps[:, 4, 0:TB * NE].rearrange("p (t e) -> p t e", t=TB)
                st.did(dve.tensor_reduce(gmax[:, :], lg, AX, ALU.max))
                st.wait()
                dve.tensor_tensor(gw[:, :, 1:], lg, gmax[:, :].unsqueeze(2).broadcast_to([P, TB, NE]),
                                  ALU.subtract).then_inc(logit_made, 1)
                return st.n

            def gate_weights(c, at):
                st = Steps(dve, dve_p, c * STEPS_P)
                st.n = at
                await_ge(dve, gexp_made, c + 1)
                st.did(dve.tensor_reduce(gsum[:, :], gw[:, :, 1:], AX, ALU.add))
                st.wait()
                st.did(dve.reciprocal(gsum[:, :], gsum[:, :]))
                st.wait()
                dve.tensor_tensor(gw[:, :, 1:], gw[:, :, 1:],
                                  gsum[:, :].unsqueeze(2).broadcast_to([P, TB, NE]), ALU.mult)\
                    .then_inc(gw_made, 1)
                await_ge(dve, gw_turned, c + 1)
                dve.tensor_copy(gateT[0:NE, :], ps[0:NE, 5, :]).then_inc(gateT_kept, 1)
                return st.n

            def keep_hidden(c, e, s):
                await_ge(dve, hid_done, CI * (NE * c + e) + 1)
                dve.tensor_scalar(hT[:, s, 0, :], ps[:, 6, :], vecs[:, bass.ds(B1 + CI * e, 1)],
                                  None, ALU.add).then_inc(hid_read, 1)

            def await_mix(c, x, half):
                await_ge(dve, exp_done, TB * ((NE + 1) * c + x) + 2 * half + 2)
                await_ge(dve, acc_made, TB * (NX * c + x) + 2 * half + 2)

            def mix(c, x, t):
                dve.scalar_tensor_tensor(acc[:, t, :], ps[:, 4 + t // 2, (t % 2) * D:(t % 2 + 1) * D],
                                         gw[:, t, bass.ds(x, 1)], acc[:, t, :],
                                         ALU.mult, ALU.add).then_inc(acc_made, 1)

            def last_mix(c):
                for t in range(TB):
                    if t % 2 == 0:
                        await_mix(c, NE, t // 2)
                    mix(c, NE, t)
                await_ge(dve, acc_made, TB * NX * (c + 1))
                dve.nop().then_inc(acc_done, 1)

            def chunk(c, first_chunk, last_open):
                at = 0
                tiles = 1 if first_chunk else 2
                scans(c, 0, 0, 0, first_chunk)
                make_r(c)
                scans(c, 0, 0, 1, first_chunk)
                if not first_chunk and not last_open:
                    await_ge(dve, summed, NP_CHUNK)
                    for hf in range(2):
                        y = arena[:, c - 1, U0 + 2 * hf:U0 + 2 * hf + 2, :]
                        dve.tensor_tensor(y, ps[:, 4 + 2 * hf:6 + 2 * hf, :], y, ALU.add)\
                            .then_inc(y0_kept, 1)
                if last_open:
                    last_mix(c - 2)
                for q in range(2 * HEAD):
                    n, s, hf = q // 2, q // 2 % 2, q % 2
                    if q == 2:
                        scans(c, n, s, hf, first_chunk)
                    elif q > 2:
                        scan(c, n, s, hf, 1, first_chunk)
                    keep_carry(c, n, hf)
                    if not first_chunk:
                        if q == 4:
                            at = rms_norm(c - 1)
                        elif q == 6:
                            at = gate_logits(c - 1, at)
                    guard(c, n, hf)
                    if not first_chunk:
                        if q == 5:
                            keep_xmT(c - 1)
                        elif q == 7:
                            assert gate_weights(c - 1, at) == STEPS_P
                    if 2 <= q < 2 * HEAD - 1:
                        q1 = q + 1
                        scan(c, q1 // 2, q1 // 2 % 2, q1 % 2, 0, first_chunk)
                    weigh(c, n, s, hf, first_chunk and n == 0, tiles)
                    if q == 2 and not first_chunk:
                        add_norm(c - 1, last_open)
                with dve.Fori(0, STEPS) as g:
                    for q in range(2 * BODY):
                        n, s, hf = HEAD + BODY * g + q // 2, q // 2 % 2, q % 2
                        i, part = q // 3, q % 3
                        e = SLOTS * g + i
                        if q and (first_chunk or part == 1):
                            scan(c, n, s, hf, 1, first_chunk)
                        else:
                            scans(c, n, s, hf, first_chunk)
                        if part and not first_chunk:
                            await_mix(c - 1, e, part - 1)
                        keep_carry(c, n, hf)
                        if part and not first_chunk:
                            mix(c - 1, e, 2 * part - 2)
                        guard(c, n, hf)
                        if not first_chunk:
                            if part:
                                mix(c - 1, e, 2 * part - 1)
                        if q < 2 * BODY - 1 and (first_chunk or part == 0):
                            q1 = q + 1
                            scan(c, HEAD + BODY * g + q1 // 2, q1 // 2 % 2, q1 % 2, 0, first_chunk)
                        weigh(c, n, s, hf, False, tiles)

            STEPS_P = 6 + 1 + 2
            chunk(0, True, False)
            chunk(1, False, False)
            with dve.Fori(2, NB) as c:
                chunk(c, False, True)
            c = NB - 1
            for hf in range(2):
                await_ge(dve, summed, NP_CHUNK * c + 2 * (NS - 1) + hf + 1)
                dve.tensor_tensor(yg[:, 2 * hf:2 * hf + 2, :],
                                  arena[:, c, U0 + 2 * hf:U0 + 2 * hf + 2, :],
                                  arena[:, c, G0 + 2 * hf:G0 + 2 * hf + 2, :], ALU.mult)\
                    .then_inc(yg_made, 1)
            last_mix(c - 1)

            def high_w1(e, s, first=False):
                if not first:
                    await_ge(dve, w1_split, e)
                await_ge(dve, w1_loaded[s], 16 * (c * (NE // 2) + (e - s) // 2 + 1))
                high_part(dve, w1_top, w1_sb[:, s, :]).then_inc(w1_high, 1)

            def place_w1(e, s):
                await_ge(dve, w1_high, e + 1)
                dve.tensor_copy(w1_hi[:, s, :], w1_top).then_inc(w1_placed, 1)

            high_w1(0, 0, True)
            place_w1(0, 0)
            add_norm(c, True)
            at = rms_norm(c)
            keep_xmT(c)
            await_ge(dve, xmT_kept, 2 * (c + 1))
            high_part(dve, xmT_top, xmT).then_inc(h_high, 1)

            await_ge(dve, h_high, 1)
            dve.tensor_tensor(xmT_lo, xmT, xmT_top, ALU.subtract).then_inc(x_split, 1)
            at = gate_logits(c, at)
            gate_weights(c, at)

            def split_hidden(e, s, half):
                m = 2 * half
                await_ge(dve, silu_made, 3 * NE * c + 4 * e + m + 2)
                await_ge(dve, h_placed, 2 * e + half + 1)
                high_part(dve, hT_top[:, m:m + 2, :], hT[:, s, m:m + 2, :]).then_inc(h_high, 1)
                await_ge(dve, h_high, 2 * e + half + 2)
                dve.tensor_tensor(hT_lo[:, s, m:m + 2, :], hT[:, s, m:m + 2, :],
                                  hT_top[:, m:m + 2, :], ALU.subtract).then_inc(h_split, 1)

            def expert(e, s, more, first=False):
                if more:
                    high_w1(e + 1, 1 - s)
                keep_hidden(c, e, s)
                if more:
                    place_w1(e + 1, 1 - s)
                split_hidden(e, s, 0)
                await_mix(c, e, 0)
                for t in range(2):
                    mix(c, e, t)
                await_ge(dve, w2_loaded[s], 16 * (c * (NE // 2) + (e - s) // 2 + 1))
                if not first:
                    await_ge(dve, w2_split, e)
                high_part(dve, w2_top, w2_sb[:, s, :]).then_inc(w2_high, 1)
                split_hidden(e, s, 1)
                await_ge(dve, w2_high, e + 1)
                dve.tensor_copy(w2_hi[:, s, :], w2_top).then_inc(w2_placed, 1)
                await_mix(c, e, 1)
                for t in range(2, TB):
                    mix(c, e, t)

            for s in range(2):
                expert(s, s, True, s == 0)
            with dve.Fori(1, NE // 2 - 1) as g:
                for s in range(2):
                    expert(2 * g + s, s, True)
            for s in range(2):
                expert(NE - 2 + s, s, s == 0)
            last_mix(c)


_INS = ['x', 'adj', 'L0_gnn_W', 'L0_gnn_b', 'L0_ffn_w_rms1', 'L0_ffn_w_rms2', 'L0_ffn_W_in',
        'L0_ffn_conv_w', 'L0_ffn_conv_b', 'L0_ffn_W_x', 'L0_ffn_W_dt', 'L0_ffn_b_dt', 'L0_ffn_A_log',
        'L0_ffn_Dp', 'L0_ffn_W_out', 'L0_ffn_W_gate', 'L0_ffn_W1', 'L0_ffn_b1', 'L0_ffn_W2',
        'L0_ffn_b2']


def kernel(**inputs):
    import numpy as np
    import concourse.bacc as bacc
    from concourse.bass_utils import run_bass_kernel_spmd

    nc = bacc.Bacc("TRN2", target_bir_lowering=False, num_devices=1, dynamic_dma_scratch_size=1024)
    arrays, args = {}, []
    for name in _INS:
        a = np.ascontiguousarray(inputs[name])
        arrays[f"in_{name}"] = a
        args.append(nc.dram_tensor(f"in_{name}", a.shape, mybir.dt.from_np(a.dtype),
                                   kind="ExternalInput").ap())
    out = nc.dram_tensor("out_rows", inputs['x'].shape, F32, kind="ExternalOutput").ap()
    build(nc, *args, out)
    r = run_bass_kernel_spmd(nc, [arrays], core_ids=[0])
    return r.results[0]["out_rows"]
```
